# Optimizing a Trainium2 kernel written in Bass

```python
import numpy as np
import jax
import jax.numpy as jnp

def _softmax(x, axis=-1):
    return jax.nn.softmax(x, axis=axis)

def _gelu(x):
    return jax.nn.gelu(x, approximate=True)

def _silu(x):
    return jax.nn.silu(x)

def _sigmoid(x):
    return jax.nn.sigmoid(x)

def _layernorm(x, axis=-1, eps=1e-05):
    m = jnp.mean(x, axis=axis, keepdims=True)
    v = jnp.var(x, axis=axis, keepdims=True)
    return (x - m) / jnp.sqrt(v + eps)

def _scatter_add(tgt, idx, src, axis=0):
    return tgt.at[idx].add(src)

def _segment_sum(src, seg, n):
    return jax.ops.segment_sum(src, seg, n)
kernel_name = 'mk_dlrm_tower_d1_rec_r8_8a7ec1'

def setup_inputs(seed: int=0):
    np.random.seed(seed)
    _w = jnp.asarray

    def _rec_inputs():
        import jax
        import jax.numpy as jnp
        _tk = jax.random.key(seed)
        ids = jnp.stack([jax.random.randint(jax.random.fold_in(_tk, 200 + f), (2048,), 0, v, jnp.int32) for f, v in enumerate([1000, 12500, 1250, 1000, 12500, 1250, 1250, 1250, 125000, 1000, 1250, 12500, 12500, 12500, 1250, 1250, 12500, 1250, 1250, 12500, 1250, 1000, 12500, 1250, 1000, 1000])], axis=1)
        tbl_0 = 0.05 * jax.random.normal(jax.random.fold_in(_tk, 500 + 0), (1000, 128), jnp.float32)
        tbl_1 = 0.05 * jax.random.normal(jax.random.fold_in(_tk, 500 + 1), (12500, 128), jnp.float32)
        tbl_2 = 0.05 * jax.random.normal(jax.random.fold_in(_tk, 500 + 2), (1250, 128), jnp.float32)
        tbl_3 = 0.05 * jax.random.normal(jax.random.fold_in(_tk, 500 + 3), (1000, 128), jnp.float32)
        tbl_4 = 0.05 * jax.random.normal(jax.random.fold_in(_tk, 500 + 4), (12500, 128), jnp.float32)
        tbl_5 = 0.05 * jax.random.normal(jax.random.fold_in(_tk, 500 + 5), (1250, 128), jnp.float32)
        tbl_6 = 0.05 * jax.random.normal(jax.random.fold_in(_tk, 500 + 6), (1250, 128), jnp.float32)
        tbl_7 = 0.05 * jax.random.normal(jax.random.fold_in(_tk, 500 + 7), (1250, 128), jnp.float32)
        tbl_8 = 0.05 * jax.random.normal(jax.random.fold_in(_tk, 500 + 8), (125000, 128), jnp.float32)
        tbl_9 = 0.05 * jax.random.normal(jax.random.fold_in(_tk, 500 + 9), (1000, 128), jnp.float32)
        tbl_10 = 0.05 * jax.random.normal(jax.random.fold_in(_tk, 500 + 10), (1250, 128), jnp.float32)
        tbl_11 = 0.05 * jax.random.normal(jax.random.fold_in(_tk, 500 + 11), (12500, 128), jnp.float32)
        tbl_12 = 0.05 * jax.random.normal(jax.random.fold_in(_tk, 500 + 12), (12500, 128), jnp.float32)
        tbl_13 = 0.05 * jax.random.normal(jax.random.fold_in(_tk, 500 + 13), (12500, 128), jnp.float32)
        tbl_14 = 0.05 * jax.random.normal(jax.random.fold_in(_tk, 500 + 14), (1250, 128), jnp.float32)
        tbl_15 = 0.05 * jax.random.normal(jax.random.fold_in(_tk, 500 + 15), (1250, 128), jnp.float32)
        tbl_16 = 0.05 * jax.random.normal(jax.random.fold_in(_tk, 500 + 16), (12500, 128), jnp.float32)
        tbl_17 = 0.05 * jax.random.normal(jax.random.fold_in(_tk, 500 + 17), (1250, 128), jnp.float32)
        tbl_18 = 0.05 * jax.random.normal(jax.random.fold_in(_tk, 500 + 18), (1250, 128), jnp.float32)
        tbl_19 = 0.05 * jax.random.normal(jax.random.fold_in(_tk, 500 + 19), (12500, 128), jnp.float32)
        tbl_20 = 0.05 * jax.random.normal(jax.random.fold_in(_tk, 500 + 20), (1250, 128), jnp.float32)
        tbl_21 = 0.05 * jax.random.normal(jax.random.fold_in(_tk, 500 + 21), (1000, 128), jnp.float32)
        tbl_22 = 0.05 * jax.random.normal(jax.random.fold_in(_tk, 500 + 22), (12500, 128), jnp.float32)
        tbl_23 = 0.05 * jax.random.normal(jax.random.fold_in(_tk, 500 + 23), (1250, 128), jnp.float32)
        tbl_24 = 0.05 * jax.random.normal(jax.random.fold_in(_tk, 500 + 24), (1000, 128), jnp.float32)
        tbl_25 = 0.05 * jax.random.normal(jax.random.fold_in(_tk, 500 + 25), (1000, 128), jnp.float32)
        _rk = jax.random.fold_in(_tk, 7)
        r_dense_features = -0.000520686 + 1.00062 * jax.random.normal(jax.random.fold_in(_rk, 101), (2048, 128), jnp.float32)
        W_top1 = 0.0405887 * jax.random.normal(jax.random.fold_in(_tk, 801), (607, 512), jnp.float32)
        W_top2 = 0.0441942 * jax.random.normal(jax.random.fold_in(_tk, 802), (512, 256), jnp.float32)
        W_top3 = 0.0625 * jax.random.normal(jax.random.fold_in(_tk, 803), (256, 1), jnp.float32)
        b_top1 = jnp.zeros((512,), jnp.float32)
        b_top2 = jnp.zeros((256,), jnp.float32)
        return (r_dense_features, ids, tbl_0, tbl_1, tbl_2, tbl_3, tbl_4, tbl_5, tbl_6, tbl_7, tbl_8, tbl_9, tbl_10, tbl_11, tbl_12, tbl_13, tbl_14, tbl_15, tbl_16, tbl_17, tbl_18, tbl_19, tbl_20, tbl_21, tbl_22, tbl_23, tbl_24, tbl_25, W_top1, b_top1, W_top2, b_top2, W_top3)
    r_dense_features, ids, tbl_0, tbl_1, tbl_2, tbl_3, tbl_4, tbl_5, tbl_6, tbl_7, tbl_8, tbl_9, tbl_10, tbl_11, tbl_12, tbl_13, tbl_14, tbl_15, tbl_16, tbl_17, tbl_18, tbl_19, tbl_20, tbl_21, tbl_22, tbl_23, tbl_24, tbl_25, W_top1, b_top1, W_top2, b_top2, W_top3 = _rec_inputs()

    def _L0_rec_setup():
        import jax, jax.numpy as jnp
        import numpy as np
        F = 26
        N = F + 1
        _TRIU_I, _TRIU_J = np.triu_indices(N, k=1)
        key = jax.random.key(seed)
        k1, k2 = jax.random.split(key)
        B, D = (2048, 128)
        dense_features = jax.random.normal(k1, (B, D), dtype=jnp.float32)
        sparse_features = jax.random.normal(k2, (B, F, D), dtype=jnp.float32)
        return {'dense_features': dense_features, 'sparse_features': sparse_features}
    _L0_rec_all = _L0_rec_setup()
    _L0_rec_in = {k: v for k, v in _L0_rec_all.items() if k in ()}
    del _L0_rec_all
    return {'r_dense_features': r_dense_features, 'ids': ids, 'tbl_0': tbl_0, 'tbl_1': tbl_1, 'tbl_2': tbl_2, 'tbl_3': tbl_3, 'tbl_4': tbl_4, 'tbl_5': tbl_5, 'tbl_6': tbl_6, 'tbl_7': tbl_7, 'tbl_8': tbl_8, 'tbl_9': tbl_9, 'tbl_10': tbl_10, 'tbl_11': tbl_11, 'tbl_12': tbl_12, 'tbl_13': tbl_13, 'tbl_14': tbl_14, 'tbl_15': tbl_15, 'tbl_16': tbl_16, 'tbl_17': tbl_17, 'tbl_18': tbl_18, 'tbl_19': tbl_19, 'tbl_20': tbl_20, 'tbl_21': tbl_21, 'tbl_22': tbl_22, 'tbl_23': tbl_23, 'tbl_24': tbl_24, 'tbl_25': tbl_25, 'W_top1': W_top1, 'b_top1': b_top1, 'W_top2': W_top2, 'b_top2': b_top2, 'W_top3': W_top3}

def reference(r_dense_features, ids, tbl_0, tbl_1, tbl_2, tbl_3, tbl_4, tbl_5, tbl_6, tbl_7, tbl_8, tbl_9, tbl_10, tbl_11, tbl_12, tbl_13, tbl_14, tbl_15, tbl_16, tbl_17, tbl_18, tbl_19, tbl_20, tbl_21, tbl_22, tbl_23, tbl_24, tbl_25, W_top1, b_top1, W_top2, b_top2, W_top3):
    import jax
    import jax.numpy as jnp

    def _L0_rec_ref(dense_features, sparse_features):
        import jax, jax.numpy as jnp
        import numpy as np
        F = 26
        N = F + 1
        _TRIU_I, _TRIU_J = np.triu_indices(N, k=1)
        combined = jnp.concatenate([dense_features[:, None, :], sparse_features], axis=1)
        interactions = jnp.einsum('bnd,bmd->bnm', combined, combined)
        interactions_flat = interactions[:, _TRIU_I, _TRIU_J]
        return jnp.concatenate([dense_features, interactions_flat], axis=1)
    e = jnp.stack([tbl_0[ids[:, 0]], tbl_1[ids[:, 1]], tbl_2[ids[:, 2]], tbl_3[ids[:, 3]], tbl_4[ids[:, 4]], tbl_5[ids[:, 5]], tbl_6[ids[:, 6]], tbl_7[ids[:, 7]], tbl_8[ids[:, 8]], tbl_9[ids[:, 9]], tbl_10[ids[:, 10]], tbl_11[ids[:, 11]], tbl_12[ids[:, 12]], tbl_13[ids[:, 13]], tbl_14[ids[:, 14]], tbl_15[ids[:, 15]], tbl_16[ids[:, 16]], tbl_17[ids[:, 17]], tbl_18[ids[:, 18]], tbl_19[ids[:, 19]], tbl_20[ids[:, 20]], tbl_21[ids[:, 21]], tbl_22[ids[:, 22]], tbl_23[ids[:, 23]], tbl_24[ids[:, 24]], tbl_25[ids[:, 25]]], axis=1)
    z = _L0_rec_ref(r_dense_features, e)
    z = z.reshape(z.shape[0], -1)
    h = jnp.concatenate([z, r_dense_features], axis=1)
    h = jnp.maximum(h @ W_top1 + b_top1, 0.0)
    h = jnp.maximum(h @ W_top2 + b_top2, 0.0)
    y = h @ W_top3
    return y

_drawn_inputs = setup_inputs


def setup_inputs(seed=0):
    import zlib

    import numpy as np

    out = dict(_drawn_inputs(seed))
    spreads = {'b_top1': (0.0, 0.1), 'b_top2': (0.0, 0.1)}
    factors = {}
    for name, (base, spread) in spreads.items():
        noise = np.random.default_rng([zlib.crc32(name.encode()), seed]).standard_normal(out[name].shape)
        drawn = base * np.exp(spread * noise) if base else spread * noise
        out[name] = jnp.asarray(drawn.astype(out[name].dtype))
    for name, factor in factors.items():
        out[name] = (out[name] * factor).astype(out[name].dtype)
    return out
```

```python
import concourse.bass as bass
from concourse import mybir
from contextlib import ExitStack

TABLES = 26


def dlrm_tower(nc, dense, ids, tables, w_pair, w_dense, b1, w2, b2, w3, out):
    fp32 = mybir.dt.float32
    i32 = mybir.dt.int32
    ALU = mybir.AluOpType
    ACT = mybir.ActivationFunctionType

    P = 128
    D = dense.shape[1]
    N = TABLES + 1
    SLOTS = 2
    BATCH = SLOTS * P
    BATCHES = dense.shape[0] // BATCH
    LANES = 4
    GROUPS = P // LANES
    GC = LANES * N
    QF = 4
    CHUNKS = -(-N // QF)
    RG = 4
    ROUNDS = GROUPS // RG
    HALF = N // 2
    NW = N + HALF
    PAIR_N = 9
    PAIR_K = PAIR_N * HALF
    KP = N // PAIR_N
    RUN = SLOTS * GROUPS
    H1, H2 = w_dense.shape[1], w2.shape[1] // (w_dense.shape[1] // P)
    C1, C2 = H1 // P, H2 // P
    OUTS = C1 + C2
    MLP_BANKS = 3
    ROUNDS_AFTER = [[], [0, 1], [2], [3], [4], [5], [6, 7]]
    LAYER1_AFTER, LAYER2_AFTER, LAYER3_AFTER = 4, 5, 6

    def features(q):
        return range(q * QF, min(N, (q + 1) * QF))

    def chunk(i, t, q):
        return (i * SLOTS + t) * CHUNKS + q

    def layer1_of(i):
        return i * OUTS + C1

    def tiles(i, t):
        return i * SLOTS + t

    out_v = out.rearrange("b o -> o b")
    ctx = ExitStack()
    with ctx:
        def sb(name, shape, dt=fp32):
            return ctx.enter_context(nc.sbuf_tensor(name, shape, dt))

        def ps(name, shape):
            return ctx.enter_context(nc.psum_tensor(name, shape, fp32))

        def sem(name):
            return ctx.enter_context(nc.semaphore(name))

        raw_ids = sb("raw_ids", [P, SLOTS * BATCHES * TABLES], i32)
        wrap = sb("wrap", [P, SLOTS * BATCHES * TABLES], i32)
        rows_of = sb("rows_of", [P, TABLES], i32)
        last_of = sb("last_of", [P, TABLES], i32)
        index = sb("index", [P, SLOTS * BATCHES * TABLES], i32)
        index_now = [sb(f"index_now{t}", [P, TABLES], i32) for t in range(SLOTS)]
        ident = sb("ident", [P, P])
        x = [sb(f"x{t}", [P, N, D]) for t in range(SLOTS)]
        x_t = [sb(f"x_t{t}", [D, P * N]) for t in range(SLOTS)]
        prod = sb("prod", [GC, GC, SLOTS, GROUPS])
        dense_new = sb("dense_new", [D, LANES, SLOTS, GROUPS])
        dense_t = sb("dense_t", [D, BATCH])
        pairs = sb("pairs", [PAIR_K, KP, LANES, RUN])
        w_pair_sb = sb("w_pair_sb", [PAIR_K, KP, H1])
        w_dense2 = sb("w_dense2", [D, 2, H1])
        w_dense_sb = sb("w_dense_sb", [D, H1])
        w2_sb = sb("w2_sb", [P, C1, H2])
        w3_sb = sb("w3_sb", [P, C2])
        b1_sb = sb("b1_sb", [P, C1])
        b2_sb = sb("b2_sb", [P, C2])
        h1 = sb("h1", [P, C1, BATCH])
        h2 = sb("h2", [P, C2, BATCH])
        y = sb("y", [1, BATCH])

        ps_t = [ps(f"ps_t{b}", [P, QF, P]) for b in range(2)]
        ps_g = [ps(f"ps_g{b}", [P, 512]) for b in range(2)]
        ps_h = [ps(f"ps_h{b}", [P, 512]) for b in range(MLP_BANKS)]
        ps_y = ps("ps_y", [P, 512])

        scratch = nc.dram_tensor("scratch", (LANES, N, NW, RUN), fp32, kind="Internal").ap()

        ids_in = sem("ids_in")
        index_ready = sem("index_ready")
        index_step = sem("index_step")
        ident_step = sem("ident_step")
        weights_in = sem("weights_in")
        w_summed = sem("w_summed")
        dense_in = [sem(f"dense_in{t}") for t in range(SLOTS)]
        gathered = [[sem(f"gathered{t}_{q}") for q in range(CHUNKS)] for t in range(SLOTS)]
        gathers_begun = sem("gathers_begun")
        transposed = sem("transposed")
        x_t_ready = sem("x_t_ready")
        dense_moved = sem("dense_moved")
        rounds_done = sem("rounds_done")
        prod_ready = sem("prod_ready")
        scratch_out = sem("scratch_out")
        pairs_in = sem("pairs_in")
        hidden_done = sem("hidden_done")
        hidden_ready = sem("hidden_ready")
        y_done = sem("y_done")
        y_ready = sem("y_ready")
        y_out = sem("y_out")

        block = ctx.enter_context(nc.Block())

        @block.sync
        def _(sp):
            def load_dense(i, t):
                row = (i * SLOTS + t) * P
                sp.dma_start(x[t][:, 0, :], dense[bass.ds(row, P), :]).then_inc(dense_in[t], 16)

            def turn_pairs(i):
                sp.wait_ge(prod_ready, (i + 1) * SLOTS * ROUNDS)
                for s in range(LANES):
                    own = prod[s * N:(s + 1) * N, s * N:(s + 1) * N, :, :].rearrange("n m t g -> n m (t g)")
                    sp.dma_start(scratch[s, :, 0:N, :], own).then_inc(scratch_out, 16)
                    sp.dma_start(scratch[s, :, N:NW, :], own[:, 0:HALF, :]).then_inc(scratch_out, 16)
                sp.wait_ge(scratch_out, (i + 1) * 2 * LANES * 16)

            def load_pairs(i):
                for n in range(N):
                    k, r = divmod(n, PAIR_N)
                    sp.dma_start(pairs[r * HALF:(r + 1) * HALF, k, :, :],
                                 scratch[:, n, n + 1:n + 1 + HALF, :].rearrange("s d r -> d s r")
                                 ).then_inc(pairs_in, 16)

            def store_y(i):
                sp.wait_ge(y_ready, i + 1)
                sp.dma_start(out_v[:, bass.ds(i * BATCH, BATCH)], y[:, :]).then_inc(y_out, 16)

            sp.dma_start(raw_ids[:, :], ids).then_inc(ids_in, 16)
            for t in range(SLOTS):
                load_dense(0, t)
            sp.dma_start(w_dense2[:, :, :], w_dense.rearrange("(a p) h -> p a h", a=2)).then_inc(weights_in, 16)
            sp.dma_start(w_pair_sb[:, :, :], w_pair.rearrange("p (k h) -> p k h", k=KP)).then_inc(weights_in, 16)
            sp.dma_start(w2_sb[:, :, :], w2.rearrange("p (c h) -> p c h", c=C1)).then_inc(weights_in, 16)
            sp.dma_start(w3_sb[:, :], w3).then_inc(weights_in, 16)
            sp.dma_start(b1_sb[:, :], b1).then_inc(weights_in, 16)
            sp.dma_start(b2_sb[:, :], b2).then_inc(weights_in, 16)
            for t in range(SLOTS):
                sp.wait_ge(transposed, chunk(0, t, 0) + 1)
                load_dense(1, t)

            def batch_turn(i, first=False, last=False):
                if not last:
                    sp.wait_ge(transposed, chunk(i, 0, 0) + 1)
                    load_dense(i + 1, 0)
                turn_pairs(i - 1)
                if not first:
                    sp.wait_ge(hidden_done, layer1_of(i - 2))
                load_pairs(i - 1)
                if not last:
                    sp.wait_ge(transposed, chunk(i, 1, 0) + 1)
                    load_dense(i + 1, 1)
                store_y(i - 1)

            batch_turn(1, first=True)
            with sp.Fori(2, BATCHES - 1) as i:
                batch_turn(i)
            batch_turn(BATCHES - 1, last=True)
            batch_turn(BATCHES, last=True)
            sp.wait_ge(y_out, BATCHES * 16)

        @block.gpsimd
        def _(pool):
            nc.gpsimd.memset(ident[:, :], 0.0).then_inc(ident_step, 1)
            pool.wait_ge(ident_step, 1)
            nc.gpsimd.affine_select(out=ident[:, :], in_=ident[:, :], compare_op=ALU.not_equal, fill=1.0,
                                    base=0, pattern=[[-1, P]], channel_multiplier=1).then_inc(ident_step, 1)

            def gather_tile(i, t, refill):
                pool.wait_ge(index_ready, tiles(i, t) + 1)
                for q in range(CHUNKS):
                    if refill:
                        pool.wait_ge(transposed, chunk(i - 1, t, q) + 1)
                    pool.sem_inc(gathers_begun, 1)
                    for n in features(q):
                        if n > 0:
                            pool.indirect_dma_start(
                                out=x[t][:, n, :], out_offset=None, in_=tables[n - 1],
                                in_offset=bass.IndirectOffsetOnAxis(ap=index_now[t][:, n - 1:n], axis=0),
                            ).then_inc(gathered[t][q], 16)

            for t in range(SLOTS):
                gather_tile(0, t, refill=False)
            with pool.Fori(1, BATCHES) as i:
                for t in range(SLOTS):
                    gather_tile(i, t, refill=True)

        @block.vector
        def _(dve):
            for n, table in enumerate(tables):
                nc.vector.memset(rows_of[:, n:n + 1], table.shape[0])
                last = nc.vector.memset(last_of[:, n:n + 1], table.shape[0] - 1)
            last.then_inc(index_step, 1)
            dve.wait_ge(ids_in, 16)
            dve.wait_ge(index_step, 1)
            per_tile = [P, SLOTS * BATCHES, TABLES]
            tiled = lambda a: a[:, :].rearrange("p (t f) -> p t f", f=TABLES)
            sizes = rows_of[:, :].rearrange("p (o f) -> p o f", o=1).broadcast_to(per_tile)
            lasts = last_of[:, :].rearrange("p (o f) -> p o f", o=1).broadcast_to(per_tile)
            nc.vector.scalar_tensor_tensor(out=tiled(wrap), in0=tiled(raw_ids), scalar=0.0, in1=sizes,
                                           op0=ALU.is_lt, op1=ALU.mult).then_inc(index_step, 1)
            dve.wait_ge(index_step, 2)
            nc.vector.tensor_tensor(wrap[:, :], wrap[:, :], raw_ids[:, :], ALU.add).then_inc(index_step, 1)
            dve.wait_ge(index_step, 3)
            nc.vector.scalar_tensor_tensor(out=tiled(index), in0=tiled(wrap), scalar=0.0, in1=lasts,
                                           op0=ALU.max, op1=ALU.min).then_inc(index_step, 1)
            dve.wait_ge(index_step, 4)

            def hand_index(i, t):
                at = (i * SLOTS + t) * TABLES
                nc.vector.tensor_copy(index_now[t][:, :], index[:, bass.ds(at, TABLES)]).then_inc(index_ready, 1)

            for t in range(SLOTS):
                hand_index(0, t)
            dve.wait_ge(weights_in, 96)
            nc.vector.tensor_tensor(w_dense_sb[:, :], w_dense2[:, 0, :], w_dense2[:, 1, :],
                                    ALU.add).then_inc(w_summed, 1)

            def take_chunk(i, t, q, first):
                dve.wait_ge(transposed, chunk(i, t, q) + 1)
                bank = ps_t[(t * CHUNKS + q) % 2]
                fs = features(q)
                if q == 0:
                    if not first:
                        dve.wait_ge(rounds_done, (tiles(i, t) - 1) * ROUNDS)
                        if t == 0:
                            if not isinstance(i, int) or i >= 2:
                                dve.wait_ge(hidden_done, layer1_of(i - 2))
                            nc.vector.tensor_copy(dense_t[:, :], dense_new[:, :, :, :].rearrange(
                                "p s t g -> p (s t g)")).then_inc(dense_moved, 1)
                            dve.wait_ge(dense_moved, i)
                    nc.vector.tensor_copy(dense_new[:, :, t, :],
                                          bank[:, 0, :].rearrange("p (g s) -> p s g", s=LANES))
                nc.vector.tensor_copy(
                    x_t[t][:, :].rearrange("p (b n) -> p n b", n=N)[:, fs.start:fs.stop, :],
                    bank[:, 0:len(fs), :]).then_inc(x_t_ready, 1)

            def take_batch(i, first=False, last=False):
                for t in range(SLOTS):
                    for q in range(CHUNKS):
                        take_chunk(i, t, q, first)
                    if not last:
                        hand_index(i + 1, t)

            take_batch(0, first=True)
            take_batch(1)
            with dve.Fori(2, BATCHES - 1) as i:
                take_batch(i)
            take_batch(BATCHES - 1, last=True)
            dve.wait_ge(hidden_done, layer1_of(BATCHES - 2))
            dve.wait_ge(x_t_ready, chunk(BATCHES, 0, 0))
            nc.vector.tensor_copy(dense_t[:, :], dense_new[:, :, :, :].rearrange(
                "p s t g -> p (s t g)")).then_inc(dense_moved, 1)

        @block.tensor
        def _(pe):
            def transpose_chunk(i, t, q, first):
                fs = features(q)
                gathers = len(fs) - (q == 0)
                if q == 0:
                    pe.wait_ge(dense_in[t], (i + 1) * 16)
                pe.wait_ge(gathered[t][q], (i + 1) * 16 * gathers)
                if not (first and t == 0 and q < 2):
                    pe.wait_ge(x_t_ready, chunk(i, t, q) - 1)
                bank = ps_t[(t * CHUNKS + q) % 2]
                for j, n in enumerate(fs):
                    last = nc.tensor.transpose(bank[:, j, :], x[t][:, n, :], ident[:, :])
                last.then_inc(transposed, 1)

            def product_round(i, t, r, first):
                if r == 0:
                    pe.wait_ge(x_t_ready, chunk(i, t, CHUNKS))
                if not (first and t == 0 and r < 2):
                    pe.wait_ge(prod_ready, tiles(i, t) * ROUNDS + r - 1)
                for k in range(RG):
                    at = (r * RG + k) * GC
                    group = x_t[t][:, at:at + GC]
                    last = nc.tensor.matmul(ps_g[r % 2][0:GC, k * GC:(k + 1) * GC], group, group,
                                            start=True, stop=True)
                last.then_inc(rounds_done, 1)

            def hidden_bank(i, k, first):
                if not (first and k < MLP_BANKS):
                    pe.wait_ge(hidden_ready, i * OUTS + k - MLP_BANKS + 1)
                return ps_h[k % MLP_BANKS][:, 0:BATCH]

            def layer1(i, first):
                pe.wait_ge(dense_moved, i + 1)
                pe.wait_ge(pairs_in, (i + 1) * N * 16)
                for c in range(C1):
                    bank = hidden_bank(i, c, first)
                    nc.tensor.matmul(bank, w_dense_sb[:, c * P:(c + 1) * P], dense_t[:, :],
                                     start=True, stop=False)
                    for k in range(KP):
                        last = nc.tensor.matmul(bank, w_pair_sb[:, k, c * P:(c + 1) * P],
                                                pairs[:, k, :, :].rearrange("p s r -> p (s r)"),
                                                start=False, stop=(k == KP - 1))
                    last.then_inc(hidden_done, 1)

            def layer2(i, first):
                pe.wait_ge(hidden_ready, i * OUTS + C1)
                for c in range(C2):
                    bank = hidden_bank(i, C1 + c, first)
                    for k in range(C1):
                        last = nc.tensor.matmul(bank, w2_sb[:, k, c * P:(c + 1) * P], h1[:, k, :],
                                                start=(k == 0), stop=(k == C1 - 1))
                    last.then_inc(hidden_done, 1)

            def layer3(i, first):
                pe.wait_ge(hidden_ready, (i + 1) * OUTS)
                if not first:
                    pe.wait_ge(y_ready, i)
                for k in range(C2):
                    last = nc.tensor.matmul(ps_y[0:1, 0:BATCH], w3_sb[:, k:k + 1], h2[:, k, :],
                                            start=(k == 0), stop=(k == C2 - 1))
                last.then_inc(y_done, 1)

            def slot(i, t, transposes=True, products=True, mlp=True, first=False):
                for q in range(CHUNKS):
                    if transposes:
                        transpose_chunk(i, t, q, first and t < 2 and not products or first)
                    if products:
                        for r in ROUNDS_AFTER[q]:
                            if t == 0:
                                product_round(i - 1, SLOTS - 1, r, False)
                            else:
                                product_round(i, t - 1, r, first)
                    if mlp and t == SLOTS - 1:
                        prior = isinstance(i, int) and i == 1
                        if q == LAYER1_AFTER:
                            layer1(i - 1, prior)
                        if q == LAYER2_AFTER:
                            layer2(i - 1, prior)
                        if q == LAYER3_AFTER:
                            layer3(i - 1, prior)

            pe.wait_ge(ident_step, 2)
            slot(0, 0, products=False, mlp=False, first=True)
            slot(0, 1, mlp=False, first=True)
            pe.wait_ge(weights_in, 96)
            pe.wait_ge(w_summed, 1)
            slot(1, 0)
            slot(1, 1)
            with pe.Fori(2, BATCHES) as i:
                slot(i, 0)
                slot(i, 1)
            slot(BATCHES, 0, transposes=False)
            layer1(BATCHES - 1, False)
            layer2(BATCHES - 1, False)
            layer3(BATCHES - 1, False)

        @block.scalar
        def _(act):
            def take_round(i, t, r, first):
                act.wait_ge(rounds_done, tiles(i, t) * ROUNDS + r + 1)
                if t == 0 and r == 0 and not first:
                    act.wait_ge(scratch_out, i * 2 * LANES * 16)
                nc.scalar.copy(prod[:, :, t, r * RG:(r + 1) * RG].rearrange("p c k -> p k c"),
                               ps_g[r % 2][0:GC, 0:RG * GC].rearrange("p (k c) -> p k c", k=RG)
                               ).then_inc(prod_ready, 1)

            def take_hidden(i, k):
                act.wait_ge(hidden_done, i * OUTS + k + 1)
                if k < C1:
                    to, bias = h1[:, k, :], b1_sb[:, k:k + 1]
                else:
                    to, bias = h2[:, k - C1, :], b2_sb[:, k - C1:k - C1 + 1]
                nc.scalar.activation(to, ps_h[k % MLP_BANKS][:, 0:BATCH], ACT.Relu,
                                     bias=bias).then_inc(hidden_ready, 1)

            def take_y(i, first):
                act.wait_ge(y_done, i + 1)
                if not first:
                    act.wait_ge(y_out, i * 16)
                nc.scalar.copy(y[:, :].rearrange("p (t g s) -> p s t g", s=LANES, g=GROUPS),
                               ps_y[0:1, 0:BATCH].rearrange("p (s t g) -> p s t g", s=LANES, g=GROUPS)
                               ).then_inc(y_ready, 1)

            def slot(i, t, mlp=True, first=False):
                for q in range(CHUNKS):
                    for r in ROUNDS_AFTER[q]:
                        if t == 0:
                            take_round(i - 1, SLOTS - 1, r, False)
                        else:
                            take_round(i, t - 1, r, first)
                    if mlp and t == SLOTS - 1:
                        if q == LAYER1_AFTER:
                            for k in range(C1):
                                take_hidden(i - 1, k)
                        if q == LAYER2_AFTER:
                            for k in range(C1, OUTS):
                                take_hidden(i - 1, k)
                        if q == LAYER3_AFTER:
                            take_y(i - 1, isinstance(i, int) and i == 1)

            act.wait_ge(weights_in, 96)
            slot(0, 1, mlp=False, first=True)
            slot(1, 0)
            slot(1, 1)
            with act.Fori(2, BATCHES) as i:
                slot(i, 0)
                slot(i, 1)
            slot(BATCHES, 0)
            for k in range(OUTS):
                take_hidden(BATCHES - 1, k)
            take_y(BATCHES - 1, False)


def kernel(**inputs):
    import numpy as np
    import concourse.bacc as bacc
    from concourse.bass_utils import run_bass_kernel_spmd as run

    f32 = lambda name: np.ascontiguousarray(inputs[name])
    P, N = 128, TABLES + 1
    dense, ids = f32("r_dense_features"), f32("ids")
    w1, w2, w3 = f32("W_top1"), f32("W_top2"), f32("W_top3")
    D = dense.shape[1]
    pairs = N * (N - 1) // 2
    place = {}
    for a in range(N):
        for b in range(a + 1, N):
            place[a, b] = D + len(place)
    order = [place[min(n, (n + d) % N), max(n, (n + d) % N)] for n in range(N) for d in range(1, N // 2 + 1)]
    K = N // 9
    w_pair = w1[np.array(order)].reshape(K, pairs // K, -1).transpose(1, 0, 2).reshape(pairs // K, -1)
    w_dense = np.concatenate([w1[:D], w1[D + pairs:]])
    tall = lambda a: a.reshape(a.shape[0] // P, P, -1).transpose(1, 0, 2).reshape(P, -1)
    given = {"dense": dense, "ids": tall(ids)}
    given |= {f"tbl_{f}": f32(f"tbl_{f}") for f in range(TABLES)}
    given |= {"w_pair": w_pair, "w_dense": w_dense, "b1": tall(f32("b_top1")), "w2": tall(w2),
              "b2": tall(f32("b_top2")), "w3": tall(w3)}

    nc = bacc.Bacc("TRN2", target_bir_lowering=False, num_devices=1)
    arrays, aps = {}, {}
    for name, a in given.items():
        arrays[name] = np.ascontiguousarray(a)
        aps[name] = nc.dram_tensor(name, a.shape, mybir.dt.from_np(a.dtype), kind="ExternalInput").ap()
    out = nc.dram_tensor("y_out", (dense.shape[0], 1), mybir.dt.float32, kind="ExternalOutput").ap()
    tables = [aps[f"tbl_{f}"] for f in range(TABLES)]
    dlrm_tower(nc, aps["dense"], aps["ids"], tables, aps["w_pair"], aps["w_dense"], aps["b1"], aps["w2"],
               aps["b2"], aps["w3"], out)
    r = run(nc, [arrays], core_ids=[0])
    return r.results[0]["y_out"]
```

```python
import concourse.bass as bass
from concourse import mybir
from contextlib import ExitStack

TABLES = 26


def dlrm_tower(nc, dense, ids, tables, hot_ids, hot_tables, w_pair, w_dense, b1, w2, b2, w3, out):
    fp32 = mybir.dt.float32
    i32 = mybir.dt.int32
    ALU = mybir.AluOpType
    ACT = mybir.ActivationFunctionType
    fp32r = mybir.dt.float32r

    P = 128
    D = dense.shape[1]
    GATHERED, HOT = len(tables), len(hot_tables)
    NG = GATHERED + 1
    N = NG + HOT
    SLOTS = 2
    BATCH = SLOTS * P
    BATCHES = dense.shape[0] // BATCH
    LANES = 4
    GROUPS = P // LANES
    GC = LANES * N
    QF = 4
    CHUNKS = -(-NG // QF)
    CUTS = [NG * q // CHUNKS for q in range(CHUNKS + 1)]
    RG = 4
    ROUNDS = GROUPS // RG
    HALF = N // 2
    NW = N + HALF
    PAIR_N = 9
    PAIR_K = PAIR_N * HALF
    KP = N // PAIR_N
    RUN = SLOTS * GROUPS
    H1, H2 = w_dense.shape[1], w2.shape[1] // (w_dense.shape[1] // P)
    C1, C2 = H1 // P, H2 // P
    OUTS = C1 + C2
    MLP_BANKS = 3
    HOT_ROWS = hot_tables[0].shape[0]
    HC = -(-HOT_ROWS // P)
    HR = HOT_ROWS // HC
    HP = 2
    PAIRS = HOT // HP
    ROUNDS_AFTER = [[[0, 1], [2, 3, 4], [5, 6, 7], [], [], []],
                    [[], [], [0, 1, 2], [3, 4, 5], [6, 7], []]]
    LOOKUPS_AFTER = [[[], [], [], [0], [], [1]],
                     [[], [2], [], [], [], []]]
    LAYER1_AFTER, LAYER23_AFTER = 4, 5
    MARKS_AFTER = [[[(1, 4, 8)], [], [], [(2, 0, 3)], [(2, 3, 6)], [(2, 6, 8)]],
                   [[], [(0, 0, 2)], [(0, 2, 4)], [(0, 4, 6)], [(0, 6, 8)], [(1, 0, 4)]]]
    BUFFER = [0, 1, 0]
    LAST_USER = [1, 3, 2]
    assert CHUNKS == 6 and PAIRS == 3 and HC == 8 and HR * HC == HOT_ROWS and HOT == PAIRS * HP
    assert all(table.shape[0] == HOT_ROWS for table in hot_tables)

    def features(q):
        return range(CUTS[q], CUTS[q + 1])

    def chunk(i, t, q):
        return (i * SLOTS + t) * CHUNKS + q

    def layer1_of(i):
        return i * OUTS + C1

    def tiles(i, t):
        return i * SLOTS + t

    out_v = out.rearrange("b o -> o b")
    ctx = ExitStack()
    with ctx:
        def sb(name, shape, dt=fp32):
            return ctx.enter_context(nc.sbuf_tensor(name, shape, dt))

        def ps(name, shape):
            return ctx.enter_context(nc.psum_tensor(name, shape, fp32))

        def sem(name):
            return ctx.enter_context(nc.semaphore(name))

        raw_ids = sb("raw_ids", [P, SLOTS * BATCHES * GATHERED], i32)
        wrap = sb("wrap", [P, SLOTS * BATCHES * GATHERED], i32)
        rows_of = sb("rows_of", [P, GATHERED], i32)
        last_of = sb("last_of", [P, GATHERED], i32)
        index = sb("index", [P, SLOTS * BATCHES * GATHERED], i32)
        index_now = [sb(f"index_now{t}", [P, GATHERED], i32) for t in range(SLOTS)]
        ident = sb("ident", [P, P])
        x = [sb(f"x{t}", [P, NG, D]) for t in range(SLOTS)]
        x_t = [sb(f"x_t{t}", [D, P * N]) for t in range(SLOTS)]
        prod_store = sb("prod_store", [P, GC * SLOTS * GROUPS])
        prod = prod_store[0:GC, :].rearrange("p (c t g) -> p c t g", c=GC, t=SLOTS)
        hot_raw = prod_store[0:HR, 0:HOT * HC * D].rearrange("p (h x) -> p h x", h=HOT)
        hot_hi = sb("hot_hi", [HR, HOT, HC * D], fp32r)
        hot_lo = sb("hot_lo", [HR, HOT, HC * D], fp32r)
        hot_index_raw = x_t[0][0:HOT, 0:SLOTS * BATCHES * P].bitcast(i32)
        wrap_hot = x_t[1][0:HOT, 0:SLOTS * BATCHES * P].bitcast(i32)
        hot_index = sb("hot_index", [P, SLOTS * BATCHES * P], fp32r)
        pick_raw = sb("pick_raw", [P, HOT, P])
        pick = sb("pick", [P, HOT, P], fp32r)
        row_of = sb("row_of", [HR, HC], i32)
        row_number = sb("row_number", [HR, HC])
        marks = [sb(f"marks{b}", [HR, HC, HP * BATCH], fp32r) for b in range(2)]
        dense_new = sb("dense_new", [D, LANES, SLOTS, GROUPS])
        dense_t = sb("dense_t", [D, BATCH])
        pairs = sb("pairs", [PAIR_K, KP, LANES, RUN])
        pairs_last = sb("pairs_last", [PAIR_K, KP, LANES, RUN])
        w_pair_sb = sb("w_pair_sb", [PAIR_K, KP, H1])
        w_dense2 = sb("w_dense2", [D, 2, H1])
        w_dense_sb = sb("w_dense_sb", [D, H1])
        w2_sb = sb("w2_sb", [P, C1, H2])
        w3_sb = sb("w3_sb", [P, C2])
        b1_sb = sb("b1_sb", [P, C1])
        b2_sb = sb("b2_sb", [P, C2])
        h1 = sb("h1", [P, C1, BATCH])
        h2 = sb("h2", [P, C2, BATCH])
        y = sb("y", [1, BATCH])

        ps_t = [ps(f"ps_t{b}", [P, QF, P]) for b in range(2)]
        ps_g = [ps(f"ps_g{b}", [P, 512]) for b in range(2)]
        ps_h = [ps(f"ps_h{b}", [P, 512]) for b in range(MLP_BANKS)]
        ps_y = ps_h[0]
        ps_s = ps("ps_s", [P, HP * BATCH])
        ps_last = ps_h + [ps_s]

        scratch = nc.dram_tensor("scratch", (LANES, N + 1, NW, RUN), fp32, kind="Internal").ap()

        ids_in = sem("ids_in")
        index_ready = sem("index_ready")
        index_step = sem("index_step")
        ident_step = sem("ident_step")
        weights_in = sem("weights_in")
        w_summed = sem("w_summed")
        hot_ids_in = sem("hot_ids_in")
        hot_in = [sem(f"hot_in{h}") for h in range(HOT)]
        hot_hi_ready = sem("hot_hi_ready")
        hot_lo_ready = sem("hot_lo_ready")
        rows_numbered = sem("rows_numbered")
        pick_ready = sem("pick_ready")
        hot_step = sem("hot_step")
        hot_zeroed = sem("hot_zeroed")
        spread_done = sem("spread_done")
        marks_ready = sem("marks_ready")
        marks_read = sem("marks_read")
        hot_taken = sem("hot_taken")
        dense_in = [sem(f"dense_in{t}") for t in range(SLOTS)]
        gathered = [[sem(f"gathered{t}_{q}") for q in range(CHUNKS)] for t in range(SLOTS)]
        gathers_begun = sem("gathers_begun")
        transposed = sem("transposed")
        x_t_ready = sem("x_t_ready")
        dense_moved = sem("dense_moved")
        rounds_done = sem("rounds_done")
        prod_ready = sem("prod_ready")
        scratch_out = sem("scratch_out")
        pairs_in = sem("pairs_in")
        pairs_last_in = [sem(f"pairs_last_in{k}") for k in range(KP)]
        hidden_done = sem("hidden_done")
        hidden_ready = sem("hidden_ready")
        y_done = sem("y_done")
        y_ready = sem("y_ready")
        y_out = sem("y_out")

        block = ctx.enter_context(nc.Block())

        @block.sync
        def _(sp):
            def load_dense(i, t):
                row = (i * SLOTS + t) * P
                sp.dma_start(x[t][:, 0, :], dense[bass.ds(row, P), :]).then_inc(dense_in[t], 16)

            def turn_pairs(i, first=False):
                sp.wait_ge(prod_ready, (i + 1) * SLOTS * ROUNDS)
                if not first:
                    sp.wait_ge(pairs_in, i * KP * LANES * 16)
                for s in range(LANES):
                    own = prod[s * N:(s + 1) * N, s * N:(s + 1) * N, :, :].rearrange("n m t g -> n m (t g)")
                    sp.dma_start(scratch[s, 0:N, 0:N, :], own).then_inc(scratch_out, 16)
                    sp.dma_start(scratch[s, 0:N, N:NW, :], own[:, 0:HALF, :]).then_inc(scratch_out, 16)
                sp.wait_ge(scratch_out, (i + 1) * 2 * LANES * 16)

            def load_pairs(i, to, loaded):
                flat = scratch.rearrange("s n m r -> s (n m) r")
                for k in range(KP):
                    for s in range(LANES):
                        at = k * PAIR_N * (NW + 1) + 1
                        rows = flat[s, at:at + PAIR_N * (NW + 1), :].rearrange(
                            "(n m) r -> n m r", m=NW + 1)[:, 0:HALF, :]
                        sp.dma_start(to[:, k, s, :], rows).then_inc(loaded[k], 16)

            def store_y(i):
                sp.wait_ge(y_ready, i + 1)
                sp.dma_start(out_v[:, bass.ds(i * BATCH, BATCH)], y[:, :]).then_inc(y_out, 16)

            sp.dma_start(raw_ids[:, :], ids).then_inc(ids_in, 16)
            sp.dma_start(hot_index_raw[:, :], hot_ids).then_inc(hot_ids_in, 16)
            for t in range(SLOTS):
                load_dense(0, t)
            for h, table in enumerate(hot_tables):
                sp.dma_start(hot_raw[:, h, :], table.rearrange("(p c) d -> p (c d)", c=HC)).then_inc(hot_in[h], 16)
            sp.dma_start(w_dense2[:, :, :], w_dense.rearrange("(a p) h -> p a h", a=2)).then_inc(weights_in, 16)
            sp.dma_start(w_pair_sb[:, :, :], w_pair.rearrange("p (k h) -> p k h", k=KP)).then_inc(weights_in, 16)
            sp.dma_start(w2_sb[:, :, :], w2.rearrange("p (c h) -> p c h", c=C1)).then_inc(weights_in, 16)
            sp.dma_start(w3_sb[:, :], w3).then_inc(weights_in, 16)
            sp.dma_start(b1_sb[:, :], b1).then_inc(weights_in, 16)
            sp.dma_start(b2_sb[:, :], b2).then_inc(weights_in, 16)
            for t in range(SLOTS):
                sp.wait_ge(transposed, chunk(0, t, 0) + 1)
                load_dense(1, t)

            def batch_turn(i, first=False, last=False):
                if not last:
                    sp.wait_ge(transposed, chunk(i, 0, 0) + 1)
                    load_dense(i + 1, 0)
                turn_pairs(i - 1, first)
                if not first:
                    sp.wait_ge(hidden_done, layer1_of(i - 2))
                load_pairs(i - 1, pairs, [pairs_in] * KP)
                if not last:
                    sp.wait_ge(transposed, chunk(i, 1, 0) + 1)
                    load_dense(i + 1, 1)
                    store_y(i - 1)

            batch_turn(1, first=True)
            with sp.Fori(2, BATCHES - 1) as i:
                batch_turn(i)
            batch_turn(BATCHES - 1, last=True)
            turn_pairs(BATCHES - 1)
            load_pairs(BATCHES - 1, pairs_last, pairs_last_in)
            store_y(BATCHES - 2)
            store_y(BATCHES - 1)
            sp.wait_ge(y_out, BATCHES * 16)

        @block.gpsimd
        def _(pool):
            nc.gpsimd.memset(hot_index[:, :].bitcast(fp32), 0.0).then_inc(hot_zeroed, 1)
            nc.gpsimd.memset(ident[:, :], 0.0).then_inc(ident_step, 1)
            pool.wait_ge(ident_step, 1)
            nc.gpsimd.affine_select(out=ident[:, :], in_=ident[:, :], compare_op=ALU.not_equal, fill=1.0,
                                    base=0, pattern=[[-1, P]], channel_multiplier=1).then_inc(ident_step, 1)
            nc.gpsimd.iota(row_of[:, :], pattern=[[1, HC]], base=0, channel_multiplier=HC).then_inc(rows_numbered, 1)
            nc.gpsimd.memset(pick_raw[:, :, :], 0.0).then_inc(ident_step, 1)
            pool.wait_ge(ident_step, 3)
            nc.gpsimd.affine_select(out=pick_raw[:, :, :], in_=pick_raw[:, :, :], compare_op=ALU.not_equal,
                                    fill=1.0, base=0, pattern=[[-1, HOT], [0, P]],
                                    channel_multiplier=1).then_inc(ident_step, 1)

            def gather_tile(i, t, refill):
                pool.wait_ge(index_ready, tiles(i, t) + 1)
                for q in range(CHUNKS):
                    if refill:
                        pool.wait_ge(transposed, chunk(i - 1, t, q) + 1)
                    pool.sem_inc(gathers_begun, 1)
                    for n in features(q):
                        if n > 0:
                            pool.indirect_dma_start(
                                out=x[t][:, n, :], out_offset=None, in_=tables[n - 1],
                                in_offset=bass.IndirectOffsetOnAxis(ap=index_now[t][:, n - 1:n], axis=0),
                            ).then_inc(gathered[t][q], 16)

            for t in range(SLOTS):
                gather_tile(0, t, refill=False)
            with pool.Fori(1, BATCHES) as i:
                for t in range(SLOTS):
                    gather_tile(i, t, refill=True)

        @block.vector
        def _(dve):
            for n, table in enumerate(tables):
                nc.vector.memset(rows_of[:, n:n + 1], table.shape[0])
                last = nc.vector.memset(last_of[:, n:n + 1], table.shape[0] - 1)
            last.then_inc(index_step, 1)
            dve.wait_ge(ids_in, 16)
            dve.wait_ge(index_step, 1)
            per_tile = [P, SLOTS * BATCHES, GATHERED]
            tiled = lambda a: a[:, :].rearrange("p (t f) -> p t f", f=GATHERED)
            sizes = rows_of[:, :].rearrange("p (o f) -> p o f", o=1).broadcast_to(per_tile)
            lasts = last_of[:, :].rearrange("p (o f) -> p o f", o=1).broadcast_to(per_tile)
            nc.vector.scalar_tensor_tensor(out=tiled(wrap), in0=tiled(raw_ids), scalar=0.0, in1=sizes,
                                           op0=ALU.is_lt, op1=ALU.mult).then_inc(index_step, 1)
            dve.wait_ge(index_step, 2)
            nc.vector.tensor_tensor(wrap[:, :], wrap[:, :], raw_ids[:, :], ALU.add).then_inc(index_step, 1)
            dve.wait_ge(index_step, 3)
            nc.vector.scalar_tensor_tensor(out=tiled(index), in0=tiled(wrap), scalar=0.0, in1=lasts,
                                           op0=ALU.max, op1=ALU.min).then_inc(index_step, 1)
            dve.wait_ge(index_step, 4)

            def hand_index(i, t):
                at = (i * SLOTS + t) * GATHERED
                nc.vector.tensor_copy(index_now[t][:, :], index[:, bass.ds(at, GATHERED)]).then_inc(index_ready, 1)

            for t in range(SLOTS):
                hand_index(0, t)

            dve.wait_ge(hot_ids_in, 16)
            hot_wrap = wrap_hot
            nc.vector.tensor_scalar(hot_wrap, hot_index_raw[:, :], 0.0, float(HOT_ROWS), ALU.is_lt,
                                    ALU.mult).then_inc(hot_step, 1)
            dve.wait_ge(hot_step, 1)
            nc.vector.tensor_tensor(hot_wrap, hot_wrap, hot_index_raw[:, :], ALU.add).then_inc(hot_step, 1)
            dve.wait_ge(hot_zeroed, 1)
            dve.wait_ge(hot_step, 2)
            nc.vector.tensor_scalar(hot_index[0:HOT, :], hot_wrap, 0.0, float(HOT_ROWS - 1), ALU.max,
                                    ALU.min).then_inc(pick_ready, 1)
            dve.wait_ge(ident_step, 4)
            nc.vector.tensor_copy(pick[:, :, :], pick_raw[:, :, :]).then_inc(pick_ready, 1)
            dve.wait_ge(rows_numbered, 1)
            nc.vector.tensor_copy(row_number[:, :], row_of[:, :]).then_inc(hot_step, 1)
            dve.wait_ge(hot_step, 3)

            def make_marks(j, pair, c0, c1, free=True):
                if c0 == 0:
                    dve.wait_ge(spread_done, j + 1)
                for c in range(c0, c1):
                    if free:
                        dve.wait_ge(marks_read, (j - LAST_USER[pair]) * HC + c + 1)
                    nc.vector.tensor_scalar(marks[BUFFER[pair]][:, c, :], ps_s[0:HR, :], row_number[:, c:c + 1], None,
                                            ALU.is_equal).then_inc(marks_ready, 1)

            def split_tables(h0, h1):
                for h in range(h0, h1):
                    dve.wait_ge(hot_hi_ready, h + 1)
                    nc.vector.tensor_tensor(hot_lo[:, h, :], hot_raw[:, h, :], hot_hi[:, h, :],
                                            ALU.subtract).then_inc(hot_lo_ready, 1)

            def take_chunk(i, t, q, first):
                dve.wait_ge(transposed, chunk(i, t, q) + 1)
                bank = ps_t[(t * CHUNKS + q) % 2]
                fs = features(q)
                if q == 0:
                    if not first:
                        dve.wait_ge(rounds_done, (tiles(i, t) - 1) * ROUNDS)
                        if t == 0:
                            if not isinstance(i, int) or i >= 2:
                                dve.wait_ge(hidden_done, layer1_of(i - 2))
                            nc.vector.tensor_copy(dense_t[:, :], dense_new[:, :, :, :].rearrange(
                                "p s t g -> p (s t g)")).then_inc(dense_moved, 1)
                            dve.wait_ge(dense_moved, i)
                    nc.vector.tensor_copy(dense_new[:, :, t, :],
                                          bank[:, 0, :].rearrange("p (g s) -> p s g", s=LANES))
                nc.vector.tensor_copy(
                    x_t[t][:, :].rearrange("p (b n) -> p n b", n=N)[:, fs.start:fs.stop, :],
                    bank[:, 0:len(fs), :]).then_inc(x_t_ready, 1)

            def take_batch(i, first=False, last=False):
                for t in range(SLOTS):
                    for q in range(CHUNKS):
                        take_chunk(i, t, q, first)
                        if first and t == 0 and q == 3:
                            make_marks(1, 1, 0, HC, free=False)
                            split_tables(HP, 2 * HP)
                        if first and t == 0 and q == 4:
                            split_tables(2 * HP, HOT)
                        for pair, c0, c1 in MARKS_AFTER[t][q]:
                            if t == 1 and not last:
                                make_marks((i + 1) * PAIRS + pair, pair, c0, c1)
                            if t == 0 and not (first and pair == 1):
                                make_marks(i * PAIRS + pair, pair, c0, c1)
                    if not last:
                        hand_index(i + 1, t)

            make_marks(0, 0, 0, HC, free=False)
            split_tables(0, HP)
            take_batch(0, first=True)
            dve.wait_ge(weights_in, 96)
            nc.vector.tensor_tensor(w_dense_sb[:, :], w_dense2[:, 0, :], w_dense2[:, 1, :],
                                    ALU.add).then_inc(w_summed, 1)
            take_batch(1)
            with dve.Fori(2, BATCHES - 1) as i:
                take_batch(i)
            take_batch(BATCHES - 1, last=True)

        @block.tensor
        def _(pe):
            def transpose_chunk(i, t, q, first):
                fs = features(q)
                gathers = len(fs) - (q == 0)
                if q == 0:
                    pe.wait_ge(dense_in[t], (i + 1) * 16)
                pe.wait_ge(gathered[t][q], (i + 1) * 16 * gathers)
                if not (first and t == 0 and q < 2):
                    pe.wait_ge(x_t_ready, chunk(i, t, q) - 1)
                bank = ps_t[(t * CHUNKS + q) % 2]
                for j, n in enumerate(fs):
                    last = nc.tensor.transpose(bank[:, j, :], x[t][:, n, :], ident[:, :])
                last.then_inc(transposed, 1)

            def product_round(i, t, r, first):
                if r == 0:
                    pe.wait_ge(x_t_ready, chunk(i, t, CHUNKS))
                    pe.wait_ge(hot_taken, (i + 1) * PAIRS)
                if not (first and t == 0 and r < 2):
                    pe.wait_ge(prod_ready, tiles(i, t) * ROUNDS + r - 1)
                for k in range(RG):
                    at = (r * RG + k) * GC
                    group = x_t[t][:, at:at + GC]
                    last = nc.tensor.matmul(ps_g[r % 2][0:GC, k * GC:(k + 1) * GC], group, group,
                                            start=True, stop=True)
                last.then_inc(rounds_done, 1)

            def spread(j, i, pair):
                if not (isinstance(j, int) and j == 0):
                    pe.wait_ge(marks_ready, j * HC)
                for k in range(HP):
                    last = nc.tensor.matmul(ps_s[:, k * BATCH:(k + 1) * BATCH], pick[:, pair * HP + k, :],
                                            hot_index[:, bass.ds(i * BATCH, BATCH)], start=True, stop=True)
                last.then_inc(spread_done, 1)

            def lookup(j, i, pair, first):
                bank = ps_g[pair % 2]
                if pair == 2:
                    pe.wait_ge(hot_taken, j - 1)
                elif not first:
                    pe.wait_ge(prod_ready, i * SLOTS * ROUNDS)
                for k in range(HP):
                    h = pair * HP + k
                    if first:
                        pe.wait_ge(hot_hi_ready, h + 1)
                        pe.wait_ge(hot_lo_ready, h + 1)
                    for c in range(HC):
                        if k == 0:
                            pe.wait_ge(marks_ready, j * HC + c + 1)
                        for part in (hot_hi, hot_lo):
                            last = nc.tensor.matmul(bank[:, k * BATCH:(k + 1) * BATCH],
                                                    part[:, h, c * D:(c + 1) * D],
                                                    marks[BUFFER[pair]][:, c, k * BATCH:(k + 1) * BATCH],
                                                    start=(c == 0 and part is hot_hi),
                                                    stop=(c == HC - 1 and part is hot_lo))
                        if k == HP - 1:
                            last.then_inc(marks_read, 1)

            def hidden_bank(i, k, first):
                if not (first and k < MLP_BANKS):
                    pe.wait_ge(hidden_ready, i * OUTS + k - MLP_BANKS + 1)
                if k == 0 and not first:
                    pe.wait_ge(y_ready, i)
                return ps_h[k % MLP_BANKS][:, 0:BATCH]

            def layer1(i, first):
                pe.wait_ge(dense_moved, i + 1)
                pe.wait_ge(pairs_in, (i + 1) * KP * LANES * 16)
                for c in range(C1):
                    bank = hidden_bank(i, c, first)
                    nc.tensor.matmul(bank, w_dense_sb[:, c * P:(c + 1) * P], dense_t[:, :],
                                     start=True, stop=False)
                    for k in range(KP):
                        last = nc.tensor.matmul(bank, w_pair_sb[:, k, c * P:(c + 1) * P],
                                                pairs[:, k, :, :].rearrange("p s r -> p (s r)"),
                                                start=False, stop=(k == KP - 1))
                    last.then_inc(hidden_done, 1)

            def layer1_last(i):
                pe.wait_ge(x_t_ready, chunk(i + 1, 0, 0))
                pe.wait_ge(hidden_ready, i * OUTS)
                pe.wait_ge(y_ready, i)
                for c in range(C1):
                    nc.tensor.matmul(ps_last[c][:, 0:BATCH], w_dense_sb[:, c * P:(c + 1) * P],
                                     dense_new[:, :, :, :].rearrange("p s t g -> p (s t g)"),
                                     start=True, stop=False)
                for k in range(KP):
                    pe.wait_ge(pairs_last_in[k], LANES * 16)
                    for c in range(C1):
                        last = nc.tensor.matmul(ps_last[c][:, 0:BATCH], w_pair_sb[:, k, c * P:(c + 1) * P],
                                                pairs_last[:, k, :, :].rearrange("p s r -> p (s r)"),
                                                start=False, stop=(k == KP - 1))
                        if k == KP - 1:
                            last.then_inc(hidden_done, 1)

            def layer2(i, first):
                for c in range(C2):
                    bank = hidden_bank(i, C1 + c, first)
                    for k in range(C1):
                        if c == 0:
                            pe.wait_ge(hidden_ready, i * OUTS + k + 1)
                        last = nc.tensor.matmul(bank, w2_sb[:, k, c * P:(c + 1) * P], h1[:, k, :],
                                                start=(k == 0), stop=(k == C1 - 1))
                    last.then_inc(hidden_done, 1)

            def layer3(i, first):
                for k in range(C2):
                    pe.wait_ge(hidden_ready, i * OUTS + C1 + k + 1)
                    last = nc.tensor.matmul(ps_y[0:1, 0:BATCH], w3_sb[:, k:k + 1], h2[:, k, :],
                                            start=(k == 0), stop=(k == C2 - 1))
                last.then_inc(y_done, 1)

            def slot(i, t, transposes=True, products=True, mlp=True, last=False):
                first = isinstance(i, int) and i == 0
                for q in range(CHUNKS):
                    if transposes:
                        transpose_chunk(i, t, q, first)
                    if t == 1 and q == CHUNKS - 1 and not last:
                        spread((i + 1) * PAIRS + 1, i + 1, 1)
                    if products:
                        for r in ROUNDS_AFTER[t][q]:
                            if t == 0:
                                product_round(i - 1, SLOTS - 1, r, False)
                            else:
                                product_round(i, t - 1, r, first)
                    if transposes:
                        for pair in LOOKUPS_AFTER[t][q]:
                            lookup(i * PAIRS + pair, i, pair, first)
                            if pair == 0:
                                spread(i * PAIRS + 2, i, 2)
                            if pair == 2 and not last:
                                spread((i + 1) * PAIRS, i + 1, 0)
                    if mlp and t == SLOTS - 1:
                        prior = isinstance(i, int) and i == 1
                        if q == LAYER1_AFTER:
                            layer1(i - 1, prior)
                        if q == LAYER23_AFTER:
                            layer2(i - 1, prior)
                            layer3(i - 1, prior)

            pe.wait_ge(pick_ready, 2)
            spread(0, 0, 0)
            spread(1, 0, 1)
            pe.wait_ge(ident_step, 2)
            slot(0, 0, products=False, mlp=False)
            slot(0, 1, mlp=False)
            pe.wait_ge(weights_in, 96)
            pe.wait_ge(w_summed, 1)
            slot(1, 0)
            slot(1, 1)
            with pe.Fori(2, BATCHES - 1) as i:
                slot(i, 0)
                slot(i, 1)
            slot(BATCHES - 1, 0)
            slot(BATCHES - 1, 1, mlp=False, last=True)
            slot(BATCHES, 0, transposes=False)
            layer1(BATCHES - 2, False)
            layer2(BATCHES - 2, False)
            layer3(BATCHES - 2, False)
            layer1_last(BATCHES - 1)
            layer2(BATCHES - 1, False)
            layer3(BATCHES - 1, False)

        @block.scalar
        def _(act):
            def take_round(i, t, r, first):
                act.wait_ge(rounds_done, tiles(i, t) * ROUNDS + r + 1)
                if t == 0 and r == 0 and not first:
                    act.wait_ge(scratch_out, i * 2 * LANES * 16)
                nc.scalar.copy(prod[:, :, t, r * RG:(r + 1) * RG].rearrange("p c k -> p k c"),
                               ps_g[r % 2][0:GC, 0:RG * GC].rearrange("p (k c) -> p k c", k=RG)
                               ).then_inc(prod_ready, 1)

            def take_hidden(i, k, banks=ps_h):
                act.wait_ge(hidden_done, i * OUTS + k + 1)
                if k < C1:
                    to, bias = h1[:, k, :], b1_sb[:, k:k + 1]
                else:
                    to, bias = h2[:, k - C1, :], b2_sb[:, k - C1:k - C1 + 1]
                nc.scalar.activation(to, banks[k % len(banks)][:, 0:BATCH], ACT.Relu,
                                     bias=bias).then_inc(hidden_ready, 1)

            def take_y(i, first):
                act.wait_ge(y_done, i + 1)
                if not first:
                    act.wait_ge(y_out, i * 16)
                nc.scalar.copy(y[:, :].rearrange("p (t g s) -> p s t g", s=LANES, g=GROUPS),
                               ps_y[0:1, 0:BATCH].rearrange("p (s t g) -> p s t g", s=LANES, g=GROUPS)
                               ).then_inc(y_ready, 1)

            def take_lookup(j, pair):
                act.wait_ge(marks_read, (j + 1) * HC)
                n = NG + pair * HP
                for t in range(SLOTS):
                    last = nc.scalar.copy(
                        x_t[t][:, :].rearrange("p (b n) -> p n b", n=N)[:, n:n + HP, :],
                        ps_g[pair % 2][:, :].rearrange("p (k t b) -> p t k b", k=HP, t=SLOTS)[:, t, :, :])
                last.then_inc(hot_taken, 1)

            def slot(i, t, products=True, lookups=True, mlp=True):
                first = isinstance(i, int) and i == 0
                for q in range(CHUNKS):
                    if products:
                        for r in ROUNDS_AFTER[t][q]:
                            if t == 0:
                                take_round(i - 1, SLOTS - 1, r, False)
                            else:
                                take_round(i, t - 1, r, first)
                    if lookups:
                        for pair in LOOKUPS_AFTER[t][q]:
                            take_lookup(i * PAIRS + pair, pair)
                    if mlp and t == SLOTS - 1:
                        if q == LAYER1_AFTER:
                            for k in range(C1):
                                take_hidden(i - 1, k)
                        if q == LAYER23_AFTER:
                            for k in range(C1, OUTS):
                                take_hidden(i - 1, k)
                            take_y(i - 1, isinstance(i, int) and i == 1)

            for h in range(HOT):
                act.wait_ge(hot_in[h], 16)
                nc.scalar.copy(hot_hi[:, h, :], hot_raw[:, h, :]).then_inc(hot_hi_ready, 1)
            act.wait_ge(weights_in, 96)
            slot(0, 0, products=False, mlp=False)
            act.wait_ge(hot_lo_ready, HOT)
            slot(0, 1, mlp=False)
            slot(1, 0)
            slot(1, 1)
            with act.Fori(2, BATCHES - 1) as i:
                slot(i, 0)
                slot(i, 1)
            slot(BATCHES - 1, 0)
            slot(BATCHES - 1, 1, mlp=False)
            slot(BATCHES, 0, lookups=False)
            for k in range(OUTS):
                take_hidden(BATCHES - 2, k)
            take_y(BATCHES - 2, False)
            for k in range(C1):
                take_hidden(BATCHES - 1, k, ps_last)
            for k in range(C1, OUTS):
                take_hidden(BATCHES - 1, k)
            take_y(BATCHES - 1, False)


def kernel(**inputs):
    import numpy as np
    import concourse.bacc as bacc
    from concourse.bass_utils import run_bass_kernel_spmd as run

    f32 = lambda name: np.ascontiguousarray(inputs[name])
    P, N = 128, TABLES + 1
    dense, ids = f32("r_dense_features"), f32("ids")
    w1, w2, w3 = f32("W_top1"), f32("W_top2"), f32("W_top3")
    D = dense.shape[1]
    pairs = N * (N - 1) // 2
    place = {}
    for a in range(N):
        for b in range(a + 1, N):
            place[a, b] = D + len(place)
    sizes = [inputs[f"tbl_{f}"].shape[0] for f in range(TABLES)]
    hot = [f for f in range(TABLES) if sizes[f] == min(sizes)]
    gathered = [f for f in range(TABLES) if f not in hot]
    column = [0] + [f + 1 for f in gathered + hot]
    around = [(column[n], column[(n + d) % N]) for n in range(N) for d in range(1, N // 2 + 1)]
    order = [place[min(pair), max(pair)] for pair in around]
    K = N // 9
    w_pair = w1[np.array(order)].reshape(K, pairs // K, -1).transpose(1, 0, 2).reshape(pairs // K, -1)
    w_dense = np.concatenate([w1[:D], w1[D + pairs:]])
    tall = lambda a: a.reshape(a.shape[0] // P, P, -1).transpose(1, 0, 2).reshape(P, -1)
    given = {"dense": dense, "ids": tall(ids[:, gathered]), "hot_ids": ids[:, hot].T}
    given |= {f"tbl_{f}": f32(f"tbl_{f}") for f in range(TABLES)}
    given |= {"w_pair": w_pair, "w_dense": w_dense, "b1": tall(f32("b_top1")), "w2": tall(w2),
              "b2": tall(f32("b_top2")), "w3": tall(w3)}

    nc = bacc.Bacc("TRN2", target_bir_lowering=False, num_devices=1)
    arrays, aps = {}, {}
    for name, a in given.items():
        arrays[name] = np.ascontiguousarray(a)
        aps[name] = nc.dram_tensor(name, a.shape, mybir.dt.from_np(a.dtype), kind="ExternalInput").ap()
    out = nc.dram_tensor("y_out", (dense.shape[0], 1), mybir.dt.float32, kind="ExternalOutput").ap()
    tables, hot_tables = [aps[f"tbl_{f}"] for f in gathered], [aps[f"tbl_{f}"] for f in hot]
    dlrm_tower(nc, aps["dense"], aps["ids"], tables, aps["hot_ids"], hot_tables, aps["w_pair"], aps["w_dense"], aps["b1"], aps["w2"],
               aps["b2"], aps["w3"], out)
    r = run(nc, [arrays], core_ids=[0])
    return r.results[0]["y_out"]
```

```python
import concourse.bass as bass
from concourse import mybir
from contextlib import ExitStack

TABLES = 26


def dlrm_tower(nc, dense, ids, tables, hot_ids, hot_tables, w_pair, w_dense, w2, small, out):
    fp32 = mybir.dt.float32
    i32 = mybir.dt.int32
    ALU = mybir.AluOpType
    ACT = mybir.ActivationFunctionType
    fp32r = mybir.dt.float32r
    fp16 = mybir.dt.float16

    P = 128
    D = dense.shape[0]
    GATHERED, HOT = len(tables), len(hot_tables)
    N = 1 + GATHERED + HOT
    SLOTS = 2
    BATCH = SLOTS * P
    BATCHES = dense.shape[1] // BATCH
    LANES = 4
    GROUPS = P // LANES
    GC = LANES * N
    QF = 4
    CHUNKS = -(-GATHERED // QF)
    CUTS = [min(q * QF, GATHERED) for q in range(CHUNKS + 1)]
    RG = 4
    ROUNDS = GROUPS // RG
    HALF = N // 2
    NW = N + HALF
    PAIR_N = 9
    PAIR_K = PAIR_N * HALF
    KP = N // PAIR_N
    RUN = SLOTS * GROUPS
    H1, H2 = w_dense.shape[1], w2.shape[1] // (w_dense.shape[1] // P)
    C1, C2 = H1 // P, H2 // P
    OUTS = C1 + C2
    MLP_BANKS = 2
    ROUND_BANKS = 4
    HP = 2
    UNITS = [range(h, min(h + HP, HOT)) for h in range(0, HOT, HP)]
    LOOKUPS = len(UNITS)
    HR = 125
    HC = [table.shape[0] // HR for table in hot_tables]
    COLS = [sum(HC[:h]) * D for h in range(HOT + 1)]
    UC = [HC[unit[0]] for unit in UNITS]
    SPLIT_ORDER = [0, 3, 1, 2]
    SPLIT_BY = [sum(len(UNITS[v]) for v in SPLIT_ORDER[:SPLIT_ORDER.index(u) + 1]) for u in range(LOOKUPS)]
    ROUNDS_AFTER = [[[0, 1, 2, 3], [4, 5, 6, 7], [], [], []],
                    [[], [], [0, 1, 2, 3], [4, 5, 6, 7], []]]
    LOOKUPS_AFTER = [[[], [], [0], [1], []],
                     [[2], [3], [], [], []]]
    INDICES_AFTER = [[[], [2], [3], [], [0]],
                     [[], [1], [], [], []]]
    LAYER1_AFTER, LAYER23_AFTER = 3, 4
    SPLIT_PAIRS_AFTER = (1, 2)
    TAKE_DENSE_AFTER, SPLIT_DENSE_AFTER = 2, 4
    MARKS_AFTER = [[[(1, 4, 8)], [], [], [(2, 0, 8)], [(3, 0, 10)]],
                   [[], [(0, 0, 4)], [(0, 4, 8)], [], [(1, 0, 4)]]]
    BUFFERS = 2
    assert PAIR_N <= HALF and CHUNKS == 5 and LOOKUPS == 4 and UC == [8, 8, 8, 10]
    assert max(table.shape[0] for table in hot_tables) <= 2048
    assert all(HC[h] == UC[u] and HC[h] * HR == hot_tables[h].shape[0]
               for u in range(LOOKUPS) for h in UNITS[u])

    def gathered_in(q):
        return range(CUTS[q], CUTS[q + 1])

    def chunk(i, t, q):
        return (i * SLOTS + t) * CHUNKS + q

    def layer1_of(i):
        return i * OUTS + C1

    def tiles(i, t):
        return i * SLOTS + t

    def marked(i, u):
        return i * sum(UC) + sum(UC[:u])

    out_v = out.rearrange("b o -> o b")
    ctx = ExitStack()
    with ctx:
        def sb(name, shape, dt=fp32):
            return ctx.enter_context(nc.sbuf_tensor(name, shape, dt))

        def ps(name, shape):
            return ctx.enter_context(nc.psum_tensor(name, shape, fp32))

        def sem(name):
            return ctx.enter_context(nc.semaphore(name))

        index = sb("index", [P, SLOTS * BATCHES * GATHERED], i32)
        index_now = [sb(f"index_now{t}", [P, GATHERED], i32) for t in range(SLOTS)]
        ident = sb("ident", [P, P])
        x = [sb(f"x{t}", [P, GATHERED, D]) for t in range(SLOTS)]
        x_t = [sb(f"x_t{t}", [D, P * N]) for t in range(SLOTS)]
        prod_store = sb("prod_store", [P, GC * SLOTS * GROUPS])
        prod = prod_store[0:GC, :].rearrange("p (c t g) -> p c t g", c=GC, t=SLOTS)
        hot_hi = sb("hot_hi", [HR, COLS[HOT]], fp32r)
        hot_lo = sb("hot_lo", [HR, COLS[HOT]], fp32r)
        IDS = SLOTS * BATCHES * GATHERED
        early = x_t[1][:, :].bitcast(i32)
        raw_ids = early[:, 0:IDS + 2 * GATHERED]
        wrap = early[:, IDS + 2 * GATHERED:2 * (IDS + GATHERED)]
        hot_raw_ids = early[0:BATCHES * HOT, 2 * (IDS + GATHERED):2 * (IDS + GATHERED) + BATCH + 2]
        wrap_hot = early[0:BATCHES * HOT, 2 * (IDS + GATHERED) + BATCH + 2:2 * (IDS + GATHERED + BATCH) + 2]
        LATE = UNITS[-1][0]
        hot_raw = [prod_store[0:HR, COLS[h]:COLS[h + 1]] for h in range(LATE)]
        behind = 2 * (IDS + GATHERED + BATCH) + 2 - COLS[LATE]
        hot_raw += [x_t[1][0:HR, behind + COLS[h]:behind + COLS[h + 1]] for h in range(LATE, HOT)]
        hot_index = sb("hot_index", [BATCHES * HOT, BATCH], fp16)
        row_of = early[0:HR, behind + COLS[HOT]:behind + COLS[HOT] + sum(UC)]
        row_number = sb("row_number", [HR, sum(UC)])
        wide = [sb(f"wide{b}", [HR, HP * BATCH], fp16) for b in range(BUFFERS)]
        marks_store = [sb(f"marks{b}", [HR, UC[b] * HP * BATCH], fp32r) for b in range(BUFFERS)]
        marks = [marks_store[u % BUFFERS][:, 0:UC[u] * len(UNITS[u]) * BATCH].rearrange("p (c x) -> p c x", c=UC[u])
                 for u in range(LOOKUPS)]
        dense_new = sb("dense_new", [D, BATCH])
        dense_hi = sb("dense_hi", [D, BATCH], fp32r)
        dense_lo = sb("dense_lo", [D, BATCH], fp32r)
        mlp_store = sb("mlp_store", [P, KP * BATCH + (C1 + C2) * BATCH + BATCH])
        pairs = mlp_store[0:PAIR_K, 0:KP * BATCH].rearrange("p (k b) -> p k b", k=KP)
        h1 = mlp_store[:, KP * BATCH:(KP + C1) * BATCH].rearrange("p (c b) -> p c b", c=C1)
        h2 = mlp_store[:, (KP + C1) * BATCH:(KP + C1 + C2) * BATCH].rearrange("p (c b) -> p c b", c=C2)
        y = mlp_store[0:1, (KP + C1 + C2) * BATCH:]
        w_dense2 = mlp_store[:, 0:2 * H1].rearrange("p (a h) -> p a h", a=2)
        w_pair_raw = mlp_store[0:PAIR_K, 2 * H1:(2 + KP) * H1].rearrange("p (k h) -> p k h", k=KP)
        pairs_hi = sb("pairs_hi", [PAIR_K, KP, BATCH], fp32r)
        pairs_lo = sb("pairs_lo", [PAIR_K, KP, BATCH], fp32r)
        w_pair_hi = sb("w_pair_hi", [PAIR_K, KP, H1], fp32r)
        w_pair_lo = sb("w_pair_lo", [PAIR_K, KP, H1], fp32r)
        w_dense_hi = sb("w_dense_hi", [D, H1], fp32r)
        w_dense_lo = sb("w_dense_lo", [D, H1], fp32r)
        w2_sb = sb("w2_sb", [P, C1, H2])
        small_sb = sb("small_sb", [P, C1 + 2 * C2])
        b1_sb, b2_sb, w3_sb = (small_sb[:, 0:C1], small_sb[:, C1:C1 + C2], small_sb[:, C1 + C2:])

        ps_t = [ps(f"ps_t{b}", [P, QF, P]) for b in range(2)]
        ps_g = [ps(f"ps_g{b}", [P, 512]) for b in range(ROUND_BANKS)]
        ps_h = [ps(f"ps_h{b}", [P, 512]) for b in range(MLP_BANKS)]
        ps_y = ps_h[0]
        ps_last = [bank[:, :, :].rearrange("p j b -> p (j b)") for bank in ps_t] + ps_h + ps_g[0:C2]

        scratch = nc.dram_tensor("scratch", (N + 1, NW, LANES, RUN), fp32, kind="Internal").ap()
        hot_scratch = nc.dram_tensor("hot_scratch", (BATCHES * HOT, BATCH), fp16, kind="Internal").ap()

        ids_in = sem("ids_in")
        index_ready = sem("index_ready")
        index_step = sem("index_step")
        ident_step = sem("ident_step")
        weights_in = sem("weights_in")
        w_step = sem("w_step")
        w_split = sem("w_split")
        hot_ids_in = sem("hot_ids_in")
        hot_in = [sem(f"hot_in{h}") for h in range(HOT)]
        hot_hi_ready = sem("hot_hi_ready")
        hot_lo_ready = sem("hot_lo_ready")
        rows_numbered = sem("rows_numbered")
        hot_index_ready = sem("hot_index_ready")
        hot_step = sem("hot_step")
        hot_index_out = sem("hot_index_out")
        wide_in = [sem(f"wide_in{b}") for b in range(BUFFERS)]
        marks_ready = sem("marks_ready")
        marks_read = sem("marks_read")
        hot_taken = sem("hot_taken")
        dense_in = sem("dense_in")
        dense_taken = sem("dense_taken")
        gathered = [[sem(f"gathered{t}_{q}") for q in range(CHUNKS)] for t in range(SLOTS)]
        gathers_begun = sem("gathers_begun")
        transposed = sem("transposed")
        x_t_ready = sem("x_t_ready")
        dense_split = sem("dense_split")
        rounds_done = sem("rounds_done")
        prod_ready = sem("prod_ready")
        scratch_out = sem("scratch_out")
        scratch_round_out = sem("scratch_round_out")
        pairs_in = [sem(f"pairs_in{k}") for k in range(KP)]
        pairs_hi_ready = sem("pairs_hi_ready")
        pairs_lo_ready = sem("pairs_lo_ready")
        hidden_done = sem("hidden_done")
        hidden_ready = sem("hidden_ready")
        y_done = sem("y_done")
        y_ready = sem("y_ready")
        y_out = sem("y_out")

        block = ctx.enter_context(nc.Block())

        @block.sync
        def _(sp):
            def load_dense(i):
                sp.dma_start(dense_new[:, :], dense[:, bass.ds(i * BATCH, BATCH)]).then_inc(dense_in, 16)

            def turn_pairs(i, first=False):
                sp.wait_ge(prod_ready, (i + 1) * SLOTS * ROUNDS)
                if not first:
                    sp.wait_ge(pairs_lo_ready, i * KP)
                for s in range(LANES):
                    own = prod[s * N:(s + 1) * N, s * N + 1:(s + 1) * N, :, :].rearrange("n m t g -> n m (t g)")
                    sp.dma_start(scratch[0:N, 1:N, s, :], own).then_inc(scratch_out, 16)
                for s in range(LANES):
                    round_rows = prod[s * N + HALF + 1:(s + 1) * N, s * N:s * N + HALF, :, :]
                    sp.dma_start(scratch[HALF + 1:N, N:NW, s, :], round_rows.rearrange("n m t g -> n m (t g)")
                                 ).then_inc(scratch_round_out, 16)
                if first:
                    sp.wait_ge(w_split, 4)
                flat = scratch.rearrange("n m s r -> (n m) (s r)")
                for k in range(KP):
                    if k == 0:
                        sp.wait_ge(scratch_out, (i + 1) * LANES * 16)
                    if k == 1:
                        sp.wait_ge(scratch_round_out, (i + 1) * LANES * 16)
                    at = k * PAIR_N * (NW + 1) + 1
                    rows = flat[at:at + PAIR_N * (NW + 1), :].rearrange(
                        "(n m) r -> n m r", m=NW + 1)[:, 0:HALF, :]
                    sp.dma_start(pairs[:, k, :], rows).then_inc(pairs_in[k], 16)

            def store_y(i):
                sp.wait_ge(y_ready, i + 1)
                sp.dma_start(out_v[:, bass.ds(i * BATCH, BATCH)], y[:, :]).then_inc(y_out, 16)

            sp.dma_start(raw_ids, ids).then_inc(ids_in, 16)
            sp.dma_start(hot_raw_ids, hot_ids).then_inc(hot_ids_in, 16)
            load_dense(0)
            for u in SPLIT_ORDER:
                for h in UNITS[u]:
                    sp.dma_start(hot_raw[h], hot_tables[h].rearrange("(p c) d -> p (c d)", c=HC[h])
                                 ).then_inc(hot_in[h], 16)
                if u == SPLIT_ORDER[0]:
                    sp.wait_ge(hot_index_ready, 1)
                    sp.dma_start(hot_scratch[:, :], hot_index[:, :]).then_inc(hot_index_out, 16)
                    for b in range(BUFFERS):
                        sp.wait_ge(wide_in[b], 16)
            sp.dma_start(w_dense2, w_dense.rearrange("(a p) h -> p a h", a=2)).then_inc(weights_in, 16)
            sp.dma_start(w_pair_raw, w_pair.rearrange("p (k h) -> p k h", k=KP)).then_inc(weights_in, 16)
            sp.dma_start(w2_sb[:, :, :], w2.rearrange("p (c h) -> p c h", c=C1)).then_inc(weights_in, 16)
            sp.dma_start(small_sb[:, :], small).then_inc(weights_in, 16)
            sp.wait_ge(dense_split, 2)
            load_dense(1)

            def batch_turn(i, first=False, last=False):
                turn_pairs(i - 1, first)
                if not last:
                    store_y(i - 1)
                    sp.wait_ge(dense_split, 2 * (i + 1))
                    load_dense(i + 1)

            batch_turn(1, first=True)
            with sp.Fori(2, BATCHES - 1) as i:
                batch_turn(i)
            batch_turn(BATCHES - 1, last=True)
            turn_pairs(BATCHES - 1)
            store_y(BATCHES - 2)
            store_y(BATCHES - 1)
            sp.wait_ge(y_out, BATCHES * 16)

        @block.gpsimd
        def _(pool):
            nc.gpsimd.memset(ident[:, :], 0.0).then_inc(ident_step, 1)
            pool.wait_ge(ident_step, 1)
            nc.gpsimd.affine_select(out=ident[:, :], in_=ident[:, :], compare_op=ALU.not_equal, fill=1.0,
                                    base=0, pattern=[[-1, P]], channel_multiplier=1).then_inc(ident_step, 1)
            for u in range(LOOKUPS):
                nc.gpsimd.iota(row_of[:, marked(0, u):marked(0, u + 1)], pattern=[[1, UC[u]]], base=0,
                               channel_multiplier=UC[u]).then_inc(rows_numbered, 1)

            def gather_tile(i, t, refill):
                pool.wait_ge(index_ready, tiles(i, t) + 1)
                for q in range(CHUNKS):
                    if refill:
                        pool.wait_ge(transposed, chunk(i - 1, t, q) + 1)
                    pool.sem_inc(gathers_begun, 1)
                    for n in gathered_in(q):
                        pool.indirect_dma_start(
                            out=x[t][:, n, :], out_offset=None, in_=tables[n],
                            in_offset=bass.IndirectOffsetOnAxis(ap=index_now[t][:, n:n + 1], axis=0),
                        ).then_inc(gathered[t][q], 16)

            for t in range(SLOTS):
                gather_tile(0, t, refill=False)
            with pool.Fori(1, BATCHES) as i:
                for t in range(SLOTS):
                    gather_tile(i, t, refill=True)

        @block.vector
        def _(dve):
            def hand_index(i, t):
                at = (i * SLOTS + t) * GATHERED
                nc.vector.tensor_copy(index_now[t][:, :], index[:, bass.ds(at, GATHERED)]).then_inc(index_ready, 1)

            tiled = lambda a: a.rearrange("p (t f) -> p t f", f=GATHERED)
            sizes = raw_ids[:, IDS:IDS + GATHERED].rearrange("p (o f) -> p o f", o=1)
            lasts = raw_ids[:, IDS + GATHERED:].rearrange("p (o f) -> p o f", o=1)
            dve.wait_ge(ids_in, 16)
            for n, (t0, t1) in enumerate(((0, SLOTS), (SLOTS, SLOTS * BATCHES))):
                cols = slice(t0 * GATHERED, t1 * GATHERED)
                like = [P, t1 - t0, GATHERED]
                nc.vector.scalar_tensor_tensor(out=tiled(wrap[:, cols]), in0=tiled(raw_ids[:, cols]), scalar=0.0,
                                               in1=sizes.broadcast_to(like), op0=ALU.is_lt, op1=ALU.mult
                                               ).then_inc(index_step, 1)
                dve.wait_ge(index_step, 3 * n + 1)
                nc.vector.tensor_tensor(wrap[:, cols], wrap[:, cols], raw_ids[:, cols], ALU.add
                                        ).then_inc(index_step, 1)
                dve.wait_ge(index_step, 3 * n + 2)
                nc.vector.scalar_tensor_tensor(out=tiled(index[:, cols]), in0=tiled(wrap[:, cols]), scalar=0.0,
                                               in1=lasts.broadcast_to(like), op0=ALU.max, op1=ALU.min
                                               ).then_inc(index_step, 1)
                dve.wait_ge(index_step, 3 * n + 3)
                if n == 0:
                    for t in range(SLOTS):
                        hand_index(0, t)

            hot_size = hot_raw_ids[:, BATCH:BATCH + 1].broadcast_to([BATCHES * HOT, BATCH])
            hot_last = hot_raw_ids[:, BATCH + 1:BATCH + 2].broadcast_to([BATCHES * HOT, BATCH])
            dve.wait_ge(hot_ids_in, 16)
            nc.vector.scalar_tensor_tensor(out=wrap_hot, in0=hot_raw_ids[:, 0:BATCH], scalar=0.0, in1=hot_size,
                                           op0=ALU.is_lt, op1=ALU.mult).then_inc(hot_step, 1)
            dve.wait_ge(hot_step, 1)
            nc.vector.tensor_tensor(wrap_hot, wrap_hot, hot_raw_ids[:, 0:BATCH], ALU.add).then_inc(hot_step, 1)
            dve.wait_ge(hot_step, 2)
            nc.vector.scalar_tensor_tensor(out=hot_index[:, :], in0=wrap_hot, scalar=0.0,
                                           in1=hot_last, op0=ALU.max, op1=ALU.min).then_inc(hot_index_ready, 1)
            dve.wait_ge(rows_numbered, LOOKUPS)
            nc.vector.tensor_copy(row_number[:, :], row_of).then_inc(hot_step, 1)
            dve.wait_ge(hot_step, 3)

            def make_marks(i, u, c0, c1, free=True):
                if c0 == 0:
                    dve.wait_ge(wide_in[u % BUFFERS], (i * (LOOKUPS // BUFFERS) + u // BUFFERS + 1) * 16)
                    if free and u % BUFFERS == 1:
                        dve.wait_ge(marks_read, marked(i - (u < BUFFERS), (u - BUFFERS) % LOOKUPS + 1))
                for c in range(c0, c1):
                    if free and u % BUFFERS == 0:
                        dve.wait_ge(marks_read, marked(i - (u < BUFFERS), (u - BUFFERS) % LOOKUPS) + c + 1)
                    at = marked(0, u) + c
                    nc.vector.tensor_scalar(marks[u][:, c, :], wide[u % BUFFERS][:, 0:len(UNITS[u]) * BATCH],
                                            row_number[:, at:at + 1], None, ALU.is_equal).then_inc(marks_ready, 1)

            def split_tables(u):
                for k, h in enumerate(UNITS[u]):
                    cols = slice(COLS[h], COLS[h + 1])
                    dve.wait_ge(hot_hi_ready, SPLIT_BY[u] - len(UNITS[u]) + k + 1)
                    nc.vector.tensor_tensor(hot_lo[:, cols], hot_raw[h], hot_hi[:, cols],
                                            ALU.subtract).then_inc(hot_lo_ready, 1)

            def split_dense(i):
                nc.vector.tensor_copy(dense_hi[:, :], dense_new[:, :]).then_inc(dense_split, 1)
                dve.wait_ge(dense_split, 2 * i + 1)
                nc.vector.tensor_tensor(dense_lo[:, :], dense_new[:, :], dense_hi[:, :],
                                        ALU.subtract).then_inc(dense_split, 1)

            def take_dense(i, first):
                dve.wait_ge(dense_in, (i + 1) * 16)
                if not first:
                    dve.wait_ge(rounds_done, tiles(i, 0) * ROUNDS)
                else:
                    dve.wait_ge(hot_lo_ready, SPLIT_BY[3])
                for t in range(SLOTS):
                    last = nc.vector.tensor_copy(
                        x_t[t][:, :].rearrange("p (g s n) -> p s g n", s=LANES, n=N)[:, :, :, 0],
                        dense_new[:, :].rearrange("p (s t g) -> p s t g", s=LANES, t=SLOTS)[:, :, t, :])
                last.then_inc(dense_taken, 1)

            def split_pairs(i):
                for k in range(KP):
                    dve.wait_ge(pairs_hi_ready, i * KP + k + 1)
                    nc.vector.tensor_tensor(pairs_lo[:, k, :], pairs[:, k, :], pairs_hi[:, k, :],
                                            ALU.subtract).then_inc(pairs_lo_ready, 1)

            def take_chunk(i, t, q, first):
                dve.wait_ge(transposed, chunk(i, t, q) + 1)
                bank = ps_t[(t * CHUNKS + q) % 2]
                fs = gathered_in(q)
                if q == 0 and not first:
                    dve.wait_ge(rounds_done, (tiles(i, t) - 1) * ROUNDS)
                nc.vector.tensor_copy(
                    x_t[t][:, :].rearrange("p (b n) -> p n b", n=N)[:, 1 + fs.start:1 + fs.stop, :],
                    bank[:, 0:len(fs), :]).then_inc(x_t_ready, 1)

            def take_batch(i, first=False, last=False):
                for t in range(SLOTS):
                    for q in range(CHUNKS):
                        take_chunk(i, t, q, first)
                        if first and t == 0 and q == 0:
                            split_tables(3)
                        if first and t == 0 and q == 1:
                            make_marks(0, 1, 0, UC[1], free=False)
                        if first and t == 0 and q == 2:
                            split_tables(1)
                        if first and t == 0 and q == 3:
                            split_tables(2)
                        for u, c0, c1 in MARKS_AFTER[t][q]:
                            if t == 1 and u < BUFFERS:
                                if not last:
                                    make_marks(i + 1, u, c0, c1)
                            elif not (first and u == 1):
                                make_marks(i, u, c0, c1)
                        if t == 0 and q == TAKE_DENSE_AFTER:
                            take_dense(i, first)
                        if not first and (t, q) == SPLIT_PAIRS_AFTER:
                            split_pairs(i - 1)
                        if t == 1 and q == SPLIT_DENSE_AFTER and not last:
                            if not first:
                                dve.wait_ge(hidden_done, layer1_of(i - 1))
                            split_dense(i)
                    if not last:
                        hand_index(i + 1, t)

            make_marks(0, 0, 0, UC[0], free=False)
            split_tables(0)
            take_batch(0, first=True)
            dve.wait_ge(weights_in, 64)
            nc.vector.tensor_tensor(w_dense2[:, 0, :], w_dense2[:, 0, :], w_dense2[:, 1, :],
                                    ALU.add).then_inc(w_step, 1)
            dve.wait_ge(w_step, 1)
            for w, hi, lo in ((w_dense2[:, 0, :], w_dense_hi[:, :], w_dense_lo[:, :]),
                              (w_pair_raw, w_pair_hi[:, :, :], w_pair_lo[:, :, :])):
                nc.vector.tensor_copy(hi, w).then_inc(w_split, 1)
                dve.wait_ge(w_split, 1 if hi.shape[0] == D else 3)
                nc.vector.tensor_tensor(lo, w, hi, ALU.subtract).then_inc(w_split, 1)
            take_batch(1)
            with dve.Fori(2, BATCHES - 1) as i:
                take_batch(i)
            take_batch(BATCHES - 1, last=True)
            dve.wait_ge(hidden_done, layer1_of(BATCHES - 2))
            split_dense(BATCHES - 1)
            split_pairs(BATCHES - 1)

        @block.tensor
        def _(pe):
            def transpose_chunk(i, t, q, first):
                fs = gathered_in(q)
                pe.wait_ge(gathered[t][q], (i + 1) * 16 * len(fs))
                if not (first and t == 0 and q < 2):
                    pe.wait_ge(x_t_ready, chunk(i, t, q) - 1)
                bank = ps_t[(t * CHUNKS + q) % 2]
                for j, n in enumerate(fs):
                    last = nc.tensor.transpose(bank[:, j, :], x[t][:, n, :], ident[:, :])
                last.then_inc(transposed, 1)

            def product_round(i, t, r, first):
                if r == 0:
                    pe.wait_ge(x_t_ready, chunk(i, t, CHUNKS))
                    pe.wait_ge(hot_taken, (i + 1) * LOOKUPS)
                    pe.wait_ge(dense_taken, i + 1)
                if not (first and t == 0 and r < ROUND_BANKS):
                    pe.wait_ge(prod_ready, tiles(i, t) * ROUNDS + r - ROUND_BANKS + 1)
                for k in range(RG):
                    at = (r * RG + k) * GC
                    group = x_t[t][:, at:at + GC]
                    last = nc.tensor.matmul(ps_g[r % ROUND_BANKS][0:GC, k * GC:(k + 1) * GC], group, group,
                                            start=True, stop=True)
                last.then_inc(rounds_done, 1)

            def lookup(i, u, first):
                bank = ps_g[u]
                if not first:
                    pe.wait_ge(prod_ready, i * SLOTS * ROUNDS - ROUND_BANKS + u + 1)
                if first:
                    pe.wait_ge(hot_hi_ready, SPLIT_BY[u])
                    pe.wait_ge(hot_lo_ready, SPLIT_BY[u])
                for k, h in enumerate(UNITS[u]):
                    for c in range(UC[u]):
                        at = COLS[h] + c * D
                        if k == 0:
                            pe.wait_ge(marks_ready, marked(i, u) + c + 1)
                        for part in (hot_hi, hot_lo):
                            last = nc.tensor.matmul(bank[:, k * BATCH:(k + 1) * BATCH], part[:, at:at + D],
                                                    marks[u][:, c, k * BATCH:(k + 1) * BATCH],
                                                    start=(c == 0 and part is hot_hi),
                                                    stop=(c == UC[u] - 1 and part is hot_lo))
                        if h == UNITS[u][-1]:
                            last.then_inc(marks_read, 1)

            def hidden_bank(i, k, first):
                if not (first and k < MLP_BANKS):
                    pe.wait_ge(hidden_ready, i * OUTS + k - MLP_BANKS + 1)
                if k == 0 and not first:
                    pe.wait_ge(y_ready, i)
                return ps_h[k % MLP_BANKS][:, 0:BATCH]

            def layer1_products(c):
                cs = slice(c * P, (c + 1) * P)
                yield [(w_dense_hi[:, cs], dense_hi[:, :]), (w_dense_lo[:, cs], dense_hi[:, :]),
                       (w_dense_hi[:, cs], dense_lo[:, :])]
                for k in range(KP):
                    yield [(w_pair_hi[:, k, cs], pairs_hi[:, k, :]), (w_pair_lo[:, k, cs], pairs_hi[:, k, :]),
                           (w_pair_hi[:, k, cs], pairs_lo[:, k, :])]

            def layer1(i, first, chunks=range(C1)):
                if first:
                    pe.wait_ge(w_split, 4)
                    pe.wait_ge(weights_in, 64)
                pe.wait_ge(dense_split, 2 * (i + 1))
                pe.wait_ge(pairs_hi_ready, (i + 1) * KP)
                pe.wait_ge(pairs_lo_ready, (i + 1) * KP)
                for c in chunks:
                    bank = hidden_bank(i, c, first)
                    products = [pair for part in layer1_products(c) for pair in part]
                    for n, (weights, features_in) in enumerate(products):
                        last = nc.tensor.matmul(bank, weights, features_in, start=(n == 0),
                                                stop=(n == len(products) - 1))
                    last.then_inc(hidden_done, 1)

            def layer1_last(i):
                pe.wait_ge(hidden_ready, i * OUTS)
                pe.wait_ge(dense_split, 2 * (i + 1))
                parts = [list(layer1_products(c)) for c in range(C1)]
                for k in range(KP + 1):
                    steps = [(c, n) for c in range(C1) for n in (0, 1)] + [(c, 2) for c in range(C1)]
                    if k == KP:
                        steps = [(c, n) for c in range(C1) for n in (0, 1, 2)]
                    for c, n in steps:
                        if k == 0 and n == 0 and ps_last[c] is ps_y:
                            pe.wait_ge(y_ready, i)
                        if k > 0 and (c, n) == (0, 0):
                            pe.wait_ge(pairs_hi_ready, i * KP + k)
                        if k > 0 and (c, n) == (0, 2):
                            pe.wait_ge(pairs_lo_ready, i * KP + k)
                        weights, features_in = parts[c][k][n]
                        last = nc.tensor.matmul(ps_last[c][:, 0:BATCH], weights, features_in,
                                                start=(k == 0 and n == 0), stop=(k == KP and n == 2))
                        if k == KP and n == 2:
                            last.then_inc(hidden_done, 1)

            def layer2(i, first, last_batch=False):
                if last_batch:
                    pe.wait_ge(prod_ready, (i + 1) * SLOTS * ROUNDS)
                for c in range(C2):
                    bank = ps_last[C1 + c][:, 0:BATCH] if last_batch else hidden_bank(i, C1 + c, first)
                    for k in range(C1):
                        if c == 0:
                            pe.wait_ge(hidden_ready, i * OUTS + k + 1)
                        last = nc.tensor.matmul(bank, w2_sb[:, k, c * P:(c + 1) * P], h1[:, k, :],
                                                start=(k == 0), stop=(k == C1 - 1))
                    last.then_inc(hidden_done, 1)

            def layer3(i, first):
                for k in range(C2):
                    pe.wait_ge(hidden_ready, i * OUTS + C1 + k + 1)
                    last = nc.tensor.matmul(ps_y[0:1, 0:BATCH], w3_sb[:, k:k + 1], h2[:, k, :],
                                            start=(k == 0), stop=(k == C2 - 1))
                last.then_inc(y_done, 1)

            def slot(i, t, transposes=True, products=True, mlp=True, last=False):
                first = isinstance(i, int) and i == 0
                for q in range(CHUNKS):
                    if transposes:
                        transpose_chunk(i, t, q, first)
                    if products:
                        for r in ROUNDS_AFTER[t][q]:
                            if t == 0:
                                product_round(i - 1, SLOTS - 1, r, False)
                            else:
                                product_round(i, t - 1, r, first)
                    if transposes:
                        for u in LOOKUPS_AFTER[t][q]:
                            lookup(i, u, first)
                    if mlp and t == SLOTS - 1:
                        prior = isinstance(i, int) and i == 1
                        if q == LAYER1_AFTER:
                            layer1(i - 1, prior)
                        if q == LAYER23_AFTER:
                            layer2(i - 1, prior)
                            layer3(i - 1, prior)

            pe.wait_ge(ident_step, 2)
            slot(0, 0, products=False, mlp=False)
            slot(0, 1, mlp=False)
            slot(1, 0)
            slot(1, 1)
            with pe.Fori(2, BATCHES - 1) as i:
                slot(i, 0)
                slot(i, 1)
            slot(BATCHES - 1, 0, last=True)
            slot(BATCHES - 1, 1, mlp=False, last=True)
            layer1(BATCHES - 2, False, range(0, 1))
            slot(BATCHES, 0, transposes=False)
            layer1(BATCHES - 2, False, range(1, C1))
            layer2(BATCHES - 2, False)
            layer3(BATCHES - 2, False)
            layer1_last(BATCHES - 1)
            layer2(BATCHES - 1, False, last_batch=True)
            layer3(BATCHES - 1, False)

        @block.scalar
        def _(act):
            def take_round(i, t, r, first):
                act.wait_ge(rounds_done, tiles(i, t) * ROUNDS + r + 1)
                if t == 0 and r == 0 and not first:
                    act.wait_ge(scratch_out, i * LANES * 16)
                    act.wait_ge(scratch_round_out, i * LANES * 16)
                nc.scalar.copy(prod[:, :, t, r * RG:(r + 1) * RG].rearrange("p c k -> p k c"),
                               ps_g[r % ROUND_BANKS][0:GC, 0:RG * GC].rearrange("p (k c) -> p k c", k=RG)
                               ).then_inc(prod_ready, 1)

            def take_hidden(i, k, banks=ps_h):
                act.wait_ge(hidden_done, i * OUTS + k + 1)
                if k < C1:
                    to, bias = h1[:, k, :], b1_sb[:, k:k + 1]
                else:
                    to, bias = h2[:, k - C1, :], b2_sb[:, k - C1:k - C1 + 1]
                nc.scalar.activation(to, banks[k % len(banks)][:, 0:BATCH], ACT.Relu,
                                     bias=bias).then_inc(hidden_ready, 1)

            def take_y(i, first):
                act.wait_ge(y_done, i + 1)
                if not first:
                    act.wait_ge(y_out, i * 16)
                nc.scalar.copy(y[:, :].rearrange("p (t g s) -> p s t g", s=LANES, g=GROUPS),
                               ps_y[0:1, 0:BATCH].rearrange("p (s t g) -> p s t g", s=LANES, g=GROUPS)
                               ).then_inc(y_ready, 1)

            def round_pairs(i):
                for k in range(KP):
                    if k == 0 and not (isinstance(i, int) and i == 0):
                        act.wait_ge(hidden_done, layer1_of(i - 1))
                    act.wait_ge(pairs_in[k], (i + 1) * 16)
                    nc.scalar.copy(pairs_hi[:, k, :], pairs[:, k, :]).then_inc(pairs_hi_ready, 1)

            def load_indices(i, u):
                if not (isinstance(i, int) and i == 0 and u < BUFFERS):
                    act.wait_ge(marks_ready, marked(i - (u < BUFFERS), (u - BUFFERS) % LOOKUPS + 1))
                hs, cols = UNITS[u], len(UNITS[u]) * BATCH
                indices = hot_scratch.rearrange("(i h) b -> i (h b)", h=HOT)[
                    bass.ds(i, 1), hs[0] * BATCH:hs[0] * BATCH + cols].broadcast_to([HR, cols])
                act.dma_start(wide[u % BUFFERS][:, 0:cols], indices).then_inc(wide_in[u % BUFFERS], 16)

            def take_lookup(i, u):
                act.wait_ge(marks_read, marked(i, u + 1))
                if isinstance(i, int) and i == 0 and u == 0:
                    act.wait_ge(hot_lo_ready, SPLIT_BY[3])
                n, size = 1 + GATHERED + UNITS[u][0], len(UNITS[u])
                for t in range(SLOTS):
                    last = nc.scalar.copy(
                        x_t[t][:, :].rearrange("p (b n) -> p n b", n=N)[:, n:n + size, :],
                        ps_g[u][:, 0:size * BATCH].rearrange("p (k t b) -> p t k b", k=size, t=SLOTS)[:, t, :, :])
                last.then_inc(hot_taken, 1)

            def slot(i, t, products=True, lookups=True, mlp=True, last=False):
                first = isinstance(i, int) and i == 0
                for q in range(CHUNKS):
                    if products:
                        for r in ROUNDS_AFTER[t][q]:
                            if t == 0:
                                take_round(i - 1, SLOTS - 1, r, False)
                            else:
                                take_round(i, t - 1, r, first)
                    if lookups:
                        for u in LOOKUPS_AFTER[t][q]:
                            take_lookup(i, u)
                        for u in INDICES_AFTER[t][q]:
                            if u >= BUFFERS:
                                load_indices(i, u)
                            elif not last:
                                load_indices(i + 1, u)
                    if (t, q) == SPLIT_PAIRS_AFTER and not (isinstance(i, int) and i == 0):
                        round_pairs(i - 1)
                    if mlp and t == SLOTS - 1:
                        if q == LAYER1_AFTER:
                            for k in range(C1):
                                take_hidden(i - 1, k)
                        if q == LAYER23_AFTER:
                            for k in range(C1, OUTS):
                                take_hidden(i - 1, k)
                            take_y(i - 1, isinstance(i, int) and i == 1)

            act.wait_ge(hot_index_out, 16)
            load_indices(0, 0)
            load_indices(0, 1)
            for h in [h for u in SPLIT_ORDER for h in UNITS[u]]:
                act.wait_ge(hot_in[h], 16)
                nc.scalar.copy(hot_hi[:, COLS[h]:COLS[h + 1]], hot_raw[h]).then_inc(hot_hi_ready, 1)
            act.wait_ge(weights_in, 64)
            slot(0, 0, products=False, mlp=False)
            act.wait_ge(hot_lo_ready, HOT)
            slot(0, 1, mlp=False)
            slot(1, 0)
            slot(1, 1)
            with act.Fori(2, BATCHES - 1) as i:
                slot(i, 0)
                slot(i, 1)
            slot(BATCHES - 1, 0, last=True)
            slot(BATCHES - 1, 1, mlp=False, last=True)
            take_hidden(BATCHES - 2, 0)
            slot(BATCHES, 0, lookups=False)
            for k in range(1, OUTS):
                take_hidden(BATCHES - 2, k)
            take_y(BATCHES - 2, False)
            round_pairs(BATCHES - 1)
            for k in range(OUTS):
                take_hidden(BATCHES - 1, k, ps_last)
            take_y(BATCHES - 1, False)


def kernel(**inputs):
    import numpy as np
    import concourse.bacc as bacc
    from concourse.bass_utils import run_bass_kernel_spmd as run

    f32 = lambda name: np.ascontiguousarray(inputs[name])
    P, N = 128, TABLES + 1
    dense, ids = inputs["r_dense_features"], f32("ids")
    w1, w2, w3 = f32("W_top1"), f32("W_top2"), f32("W_top3")
    D = dense.shape[1]
    pairs = N * (N - 1) // 2
    place = {}
    for a in range(N):
        for b in range(a + 1, N):
            place[a, b] = D + len(place)
    sizes = [inputs[f"tbl_{f}"].shape[0] for f in range(TABLES)]
    hot = sorted(range(TABLES), key=lambda f: sizes[f])[:7]
    gathered = [f for f in range(TABLES) if f not in hot]
    column = [0] + [f + 1 for f in gathered + hot]
    around = [(column[n], column[(n + d) % N]) for n in range(N) for d in range(1, N // 2 + 1)]
    order = [place[min(pair), max(pair)] for pair in around]
    K = N // 9
    w_pair = w1[np.array(order)].reshape(K, pairs // K, -1).transpose(1, 0, 2).reshape(pairs // K, -1)
    w_dense = np.concatenate([w1[:D], w1[D + pairs:]])
    tall = lambda a: a.reshape(a.shape[0] // P, P, -1).transpose(1, 0, 2).reshape(P, -1)
    rows = np.array(sizes, np.int32)
    ends = lambda fs: np.stack([rows[fs], rows[fs] - 1])
    batches = dense.shape[0] // (2 * P)
    hot_ids = ids[:, hot].reshape(batches, 2 * P, len(hot)).transpose(0, 2, 1).reshape(batches * len(hot), 2 * P)
    by_lane = dense.reshape(batches, 2, P // 4, 4, D).transpose(4, 0, 3, 1, 2).reshape(D, -1)
    given = {"dense": by_lane,
             "ids": np.concatenate([tall(ids[:, gathered]), np.tile(ends(gathered).reshape(1, -1), (P, 1))], 1),
             "hot_ids": np.concatenate([hot_ids, np.tile(ends(hot).T, (batches, 1))], 1)}
    given |= {f"tbl_{f}": f32(f"tbl_{f}") for f in range(TABLES)}
    small = np.concatenate([tall(f32("b_top1")), tall(f32("b_top2")), tall(w3)], 1)
    given |= {"w_pair": w_pair, "w_dense": w_dense, "w2": tall(w2), "small": small}

    nc = bacc.Bacc("TRN2", target_bir_lowering=False, num_devices=1)
    arrays, aps = {}, {}
    for name, a in given.items():
        arrays[name] = np.ascontiguousarray(a)
        aps[name] = nc.dram_tensor(name, a.shape, mybir.dt.from_np(a.dtype), kind="ExternalInput").ap()
    out = nc.dram_tensor("y_out", (dense.shape[0], 1), mybir.dt.float32, kind="ExternalOutput").ap()
    tables, hot_tables = [aps[f"tbl_{f}"] for f in gathered], [aps[f"tbl_{f}"] for f in hot]
    dlrm_tower(nc, aps["dense"], aps["ids"], tables, aps["hot_ids"], hot_tables, aps["w_pair"], aps["w_dense"],
               aps["w2"], aps["small"], out)
    r = run(nc, [arrays], core_ids=[0])
    return r.results[0]["y_out"]
```
